# Optimizing a Trainium2 kernel written in Bass

```python
import numpy as np
import jax
import jax.numpy as jnp

def _softmax(x, axis=-1):
    return jax.nn.softmax(x, axis=axis)

def _gelu(x):
    return jax.nn.gelu(x, approximate=True)

def _silu(x):
    return jax.nn.silu(x)

def _sigmoid(x):
    return jax.nn.sigmoid(x)

def _layernorm(x, axis=-1, eps=1e-05):
    m = jnp.mean(x, axis=axis, keepdims=True)
    v = jnp.var(x, axis=axis, keepdims=True)
    return (x - m) / jnp.sqrt(v + eps)

def _scatter_add(tgt, idx, src, axis=0):
    return tgt.at[idx].add(src)

def _segment_sum(src, seg, n):
    return jax.ops.segment_sum(src, seg, n)
kernel_name = 'mk_vit_tower_postln_d1_tok_img768_r4_ef3a3f'

def setup_inputs(seed: int=0):
    np.random.seed(seed)
    _w = jnp.asarray

    def _rec_inputs():
        import jax
        import jax.numpy as jnp
        _rk = jax.random.key(seed)
        x = -0.000356955 + 1 * jax.random.normal(jax.random.fold_in(_rk, 1), (32, 3, 64, 64), jnp.float32)
        return x
    x = _rec_inputs()

    def _L0_tok_setup():
        import jax, jax.numpy as jnp
        import numpy as np
        PATCH = 16
        EMBED = 192
        IN_DIM = PATCH * PATCH * 3

        def extract_patches(x, p):
            B, C, H, Wd = x.shape
            h, w = (H // p, Wd // p)
            xr = x.reshape(B, C, h, p, w, p)
            xr = xr.transpose(0, 2, 4, 3, 5, 1)
            return xr.reshape(B, h * w, p * p * C)
        key = jax.random.key(seed)
        kx, kw, kb = jax.random.split(key, 3)
        x = jax.random.normal(kx, (128, 3, 224, 224), dtype=jnp.float32)
        bound = 1.0 / np.sqrt(IN_DIM)
        W = jax.random.uniform(kw, (EMBED, IN_DIM), jnp.float32, -bound, bound)
        b = jax.random.uniform(kb, (EMBED,), jnp.float32, -bound, bound)
        return {'x': x, 'W': W, 'b': b}
    _L0_tok_all = _L0_tok_setup()
    _L0_tok_in = {k: v for k, v in _L0_tok_all.items() if k in ('W', 'b')}
    del _L0_tok_all

    def _L0_attn_setup():
        import jax, jax.numpy as jnp
        import numpy as np
        L = 4
        D_MODEL = 192
        D_STATE = 16
        D_CONV = 4
        EXPAND = 2
        D_INNER = EXPAND * D_MODEL
        DT_RANK = (D_MODEL + 15) // 16
        B = 2
        T = 512
        LN_EPS = 1e-05

        def _layernorm(x, g, b):
            mu = jnp.mean(x, axis=-1, keepdims=True)
            var = jnp.mean(jnp.square(x - mu), axis=-1, keepdims=True)
            return (x - mu) * jax.lax.rsqrt(var + LN_EPS) * g + b

        def _mamba_layer(x, inw, convw, convb, xpw, dtw, dtb, A_log, Dp, outw):
            Tn = x.shape[1]
            xz = jnp.einsum('btd,ed->bte', x, inw)
            xin, z = jnp.split(xz, 2, axis=-1)
            xp = jnp.pad(xin, ((0, 0), (D_CONV - 1, 0), (0, 0)))
            xc = convb
            for k in range(D_CONV):
                xc = xc + xp[:, k:k + Tn, :] * convw[:, k]
            xc = jax.nn.silu(xc)
            dbl = jnp.einsum('bti,ei->bte', xc, xpw)
            dt, Bs, Cs = jnp.split(dbl, [DT_RANK, DT_RANK + D_STATE], axis=-1)
            dt = jax.nn.softplus(jnp.einsum('btr,dr->btd', dt, dtw) + dtb)
            A = -jnp.exp(A_log)
            dA = jnp.exp(jnp.einsum('btd,dn->btdn', dt, A))
            dBu = (dt * xc)[..., None] * Bs[:, :, None, :]

            def step(h, inp):
                dA_t, dBu_t, C_t = inp
                h = dA_t * h + dBu_t
                y = jnp.einsum('bdn,bn->bd', h, C_t)
                return (h, y)
            h0 = jnp.zeros((x.shape[0], D_INNER, D_STATE), x.dtype)
            _, ys = jax.lax.scan(step, h0, (jnp.swapaxes(dA, 0, 1), jnp.swapaxes(dBu, 0, 1), jnp.swapaxes(Cs, 0, 1)))
            y = jnp.swapaxes(ys, 0, 1) + xc * Dp
            y = y * jax.nn.silu(z)
            return jnp.einsum('bti,ei->bte', y, outw)
        key = jax.random.key(seed)
        ks = jax.random.split(key, 12)
        s = 0.02
        x = jax.random.normal(ks[0], (B, T, D_MODEL), dtype=jnp.float32)
        in_proj_w = jax.random.normal(ks[1], (L, 2 * D_INNER, D_MODEL), dtype=jnp.float32) * s
        conv_w = jax.random.normal(ks[2], (L, D_INNER, D_CONV), dtype=jnp.float32) * s
        conv_b = jnp.zeros((L, D_INNER), dtype=jnp.float32)
        x_proj_w = jax.random.normal(ks[3], (L, DT_RANK + 2 * D_STATE, D_INNER), dtype=jnp.float32) * s
        dt_proj_w = jax.random.normal(ks[4], (L, D_INNER, DT_RANK), dtype=jnp.float32) * s
        dt_proj_b = jax.random.normal(ks[5], (L, D_INNER), dtype=jnp.float32) * 0.1
        A_log = jnp.log(jnp.broadcast_to(jnp.arange(1, D_STATE + 1, dtype=jnp.float32), (L, D_INNER, D_STATE)))
        D_param = jnp.ones((L, D_INNER), dtype=jnp.float32)
        out_proj_w = jax.random.normal(ks[6], (L, D_MODEL, D_INNER), dtype=jnp.float32) * s
        ln_g = jnp.ones((L, D_MODEL), dtype=jnp.float32)
        ln_b = jnp.zeros((L, D_MODEL), dtype=jnp.float32)
        return {'x': x, 'in_proj_w': in_proj_w, 'conv_w': conv_w, 'conv_b': conv_b, 'x_proj_w': x_proj_w, 'dt_proj_w': dt_proj_w, 'dt_proj_b': dt_proj_b, 'A_log': A_log, 'D_param': D_param, 'out_proj_w': out_proj_w, 'ln_g': ln_g, 'ln_b': ln_b}
    _L0_attn_all = _L0_attn_setup()
    _L0_attn_in = {k: v for k, v in _L0_attn_all.items() if k in ('in_proj_w', 'conv_w', 'conv_b', 'x_proj_w', 'dt_proj_w', 'dt_proj_b', 'A_log', 'D_param', 'out_proj_w', 'ln_g', 'ln_b')}
    del _L0_attn_all

    def _L0_ffn_setup():
        import jax, jax.numpy as jnp
        import numpy as np
        B, S, H, F, E, TOP_K = (4, 512, 192, 768, 8, 2)
        key = jax.random.key(seed)
        ks = jax.random.split(key, 6)
        x = jax.random.normal(ks[0], (B, S, H), dtype=jnp.float32)
        Wr = jax.random.normal(ks[1], (E, H), dtype=jnp.float32) * 0.02
        Wi = jax.random.normal(ks[2], (E, F, H), dtype=jnp.float32) * 0.02
        bi = jnp.zeros((E, F), dtype=jnp.float32)
        Wo = jax.random.normal(ks[3], (E, H, F), dtype=jnp.float32) * 0.02
        bo = jnp.zeros((E, H), dtype=jnp.float32)
        return {'x': x, 'Wr': Wr, 'Wi': Wi, 'bi': bi, 'Wo': Wo, 'bo': bo}
    _L0_ffn_all = _L0_ffn_setup()
    _L0_ffn_in = {k: v for k, v in _L0_ffn_all.items() if k in ('Wr', 'Wi', 'bi', 'Wo', 'bo')}
    del _L0_ffn_all
    return {'x': x, 'L0_tok_W': _L0_tok_in['W'], 'L0_tok_b': _L0_tok_in['b'], 'L0_attn_in_proj_w': _L0_attn_in['in_proj_w'], 'L0_attn_conv_w': _L0_attn_in['conv_w'], 'L0_attn_conv_b': _L0_attn_in['conv_b'], 'L0_attn_x_proj_w': _L0_attn_in['x_proj_w'], 'L0_attn_dt_proj_w': _L0_attn_in['dt_proj_w'], 'L0_attn_dt_proj_b': _L0_attn_in['dt_proj_b'], 'L0_attn_A_log': _L0_attn_in['A_log'], 'L0_attn_D_param': _L0_attn_in['D_param'], 'L0_attn_out_proj_w': _L0_attn_in['out_proj_w'], 'L0_attn_ln_g': _L0_attn_in['ln_g'], 'L0_attn_ln_b': _L0_attn_in['ln_b'], 'L0_ffn_Wr': _L0_ffn_in['Wr'], 'L0_ffn_Wi': _L0_ffn_in['Wi'], 'L0_ffn_bi': _L0_ffn_in['bi'], 'L0_ffn_Wo': _L0_ffn_in['Wo'], 'L0_ffn_bo': _L0_ffn_in['bo']}

def reference(x, L0_tok_W, L0_tok_b, L0_attn_in_proj_w, L0_attn_conv_w, L0_attn_conv_b, L0_attn_x_proj_w, L0_attn_dt_proj_w, L0_attn_dt_proj_b, L0_attn_A_log, L0_attn_D_param, L0_attn_out_proj_w, L0_attn_ln_g, L0_attn_ln_b, L0_ffn_Wr, L0_ffn_Wi, L0_ffn_bi, L0_ffn_Wo, L0_ffn_bo):
    import jax
    import jax.numpy as jnp

    def _L0_tok_ref(x, W, b):
        import jax, jax.numpy as jnp
        import numpy as np
        PATCH = 16
        EMBED = 192
        IN_DIM = PATCH * PATCH * 3

        def extract_patches(x, p):
            B, C, H, Wd = x.shape
            h, w = (H // p, Wd // p)
            xr = x.reshape(B, C, h, p, w, p)
            xr = xr.transpose(0, 2, 4, 3, 5, 1)
            return xr.reshape(B, h * w, p * p * C)
        patches = extract_patches(x, PATCH)
        return jnp.einsum('bnd,ed->bne', patches, W) + b

    def _L0_attn_ref(x, in_proj_w, conv_w, conv_b, x_proj_w, dt_proj_w, dt_proj_b, A_log, D_param, out_proj_w, ln_g, ln_b):
        import jax, jax.numpy as jnp
        import numpy as np
        L = 4
        D_MODEL = 192
        D_STATE = 16
        D_CONV = 4
        EXPAND = 2
        D_INNER = EXPAND * D_MODEL
        DT_RANK = (D_MODEL + 15) // 16
        B = 2
        T = 512
        LN_EPS = 1e-05

        def _layernorm(x, g, b):
            mu = jnp.mean(x, axis=-1, keepdims=True)
            var = jnp.mean(jnp.square(x - mu), axis=-1, keepdims=True)
            return (x - mu) * jax.lax.rsqrt(var + LN_EPS) * g + b

        def _mamba_layer(x, inw, convw, convb, xpw, dtw, dtb, A_log, Dp, outw):
            Tn = x.shape[1]
            xz = jnp.einsum('btd,ed->bte', x, inw)
            xin, z = jnp.split(xz, 2, axis=-1)
            xp = jnp.pad(xin, ((0, 0), (D_CONV - 1, 0), (0, 0)))
            xc = convb
            for k in range(D_CONV):
                xc = xc + xp[:, k:k + Tn, :] * convw[:, k]
            xc = jax.nn.silu(xc)
            dbl = jnp.einsum('bti,ei->bte', xc, xpw)
            dt, Bs, Cs = jnp.split(dbl, [DT_RANK, DT_RANK + D_STATE], axis=-1)
            dt = jax.nn.softplus(jnp.einsum('btr,dr->btd', dt, dtw) + dtb)
            A = -jnp.exp(A_log)
            dA = jnp.exp(jnp.einsum('btd,dn->btdn', dt, A))
            dBu = (dt * xc)[..., None] * Bs[:, :, None, :]

            def step(h, inp):
                dA_t, dBu_t, C_t = inp
                h = dA_t * h + dBu_t
                y = jnp.einsum('bdn,bn->bd', h, C_t)
                return (h, y)
            h0 = jnp.zeros((x.shape[0], D_INNER, D_STATE), x.dtype)
            _, ys = jax.lax.scan(step, h0, (jnp.swapaxes(dA, 0, 1), jnp.swapaxes(dBu, 0, 1), jnp.swapaxes(Cs, 0, 1)))
            y = jnp.swapaxes(ys, 0, 1) + xc * Dp
            y = y * jax.nn.silu(z)
            return jnp.einsum('bti,ei->bte', y, outw)
        for l in range(L):
            residual = x
            h = _mamba_layer(x, in_proj_w[l], conv_w[l], conv_b[l], x_proj_w[l], dt_proj_w[l], dt_proj_b[l], A_log[l], D_param[l], out_proj_w[l])
            h = _layernorm(h, ln_g[l], ln_b[l])
            x = h + residual
        return x

    def _L0_ffn_ref(x, Wr, Wi, bi, Wo, bo):
        import jax, jax.numpy as jnp
        import numpy as np
        B, S, H, F, E, TOP_K = (4, 512, 192, 768, 8, 2)
        xf = x.reshape(-1, x.shape[-1])
        router_logits = jnp.einsum('th,eh->te', xf, Wr)
        topk_vals, topk_idx = jax.lax.top_k(router_logits, TOP_K)
        routing_weights = jax.nn.softmax(topk_vals, axis=-1)
        h = jnp.einsum('th,efh->etf', xf, Wi) + bi[:, None, :]
        h = jax.nn.gelu(h, approximate=False)
        expert_out = jnp.einsum('etf,ehf->eth', h, Wo) + bo[:, None, :]
        expert_out = jnp.transpose(expert_out, (1, 0, 2))
        gathered = jnp.take_along_axis(expert_out, topk_idx[:, :, None], axis=1)
        out = jnp.einsum('tk,tkh->th', routing_weights, gathered)
        return out.reshape(x.shape)
    h = _L0_tok_ref(x, L0_tok_W, L0_tok_b)
    h = _layernorm(h + _L0_attn_ref(h, L0_attn_in_proj_w, L0_attn_conv_w, L0_attn_conv_b, L0_attn_x_proj_w, L0_attn_dt_proj_w, L0_attn_dt_proj_b, L0_attn_A_log, L0_attn_D_param, L0_attn_out_proj_w, L0_attn_ln_g, L0_attn_ln_b), axis=-1)
    h = _layernorm(h + _L0_ffn_ref(h, L0_ffn_Wr, L0_ffn_Wi, L0_ffn_bi, L0_ffn_Wo, L0_ffn_bo), axis=-1)
    return h

_drawn_inputs = setup_inputs


def setup_inputs(seed=0):
    import zlib

    import numpy as np

    out = dict(_drawn_inputs(seed))
    spreads = {'L0_attn_conv_b': (0.0, 0.1),
     'L0_attn_D_param': (1.0, 0.2),
     'L0_attn_ln_g': (1.0, 0.2),
     'L0_attn_ln_b': (0.0, 0.1),
     'L0_ffn_bi': (0.0, 0.393),
     'L0_ffn_bo': (0.0, 0.1)}
    factors = {'L0_attn_x_proj_w': 8.0,
     'L0_attn_dt_proj_w': 64.0,
     'L0_attn_dt_proj_b': 8.0,
     'L0_attn_A_log': 56.334}
    for name, (base, spread) in spreads.items():
        noise = np.random.default_rng([zlib.crc32(name.encode()), seed]).standard_normal(out[name].shape)
        drawn = base * np.exp(spread * noise) if base else spread * noise
        out[name] = jnp.asarray(drawn.astype(out[name].dtype))
    for name, factor in factors.items():
        out[name] = (out[name] * factor).astype(out[name].dtype)
    return out
```

```python
import concourse.bass as bass
from concourse import mybir
from contextlib import ExitStack

LAYERS = 4
D = 192
DI = 384
NST = 16
RANK = 12
KCONV = 4
T = 16
B = 32
G = 2
GB = B // G
GT = GB * T
NTOK = B * T
C = DI // 128
DK = D // 2
PATCH = 768
PC = PATCH // 128
EPS = 1e-5
A_LOG_MAX = 80.0
PAIRS = NST // 2
UNITS = PAIRS * C
RUNS = LAYERS * G
E = 8
F = 768
FC = F // 128
TC = NTOK // 128
SM_CONVW, SM_CONVB, SM_DTB, SM_DP = 0, 4, 5, 6
SM = 7


def tower_program(nc, patches, tok_w, tok_b, in_w, xp_w, dt_w, out_w, lngb, smalls, a_log,
                  wr, wi, bi, wo, bo, eye, sel, iota8, out):
    fp32 = mybir.dt.float32
    bf16 = mybir.dt.bfloat16
    u32 = mybir.dt.uint32
    ALU = mybir.AluOpType
    ACT = mybir.ActivationFunctionType

    RA, RH, RC, RCB = 6, 4, 4, 3

    ctx = ExitStack()
    with ctx:
        def sb(name, shape, dt=fp32):
            return ctx.enter_context(nc.sbuf_tensor(name, shape, dt))

        def pb(name, shape, dt=fp32):
            return ctx.enter_context(nc.psum_tensor(name, shape, dt))

        def sem(name):
            return ctx.enter_context(nc.semaphore(name))

        ident = sb("ident", [128, 128])
        selc = sb("selc", [128, 2 * NST])
        sel_sb = sb("sel_sb", [128, 2 * NST, 128], bf16)
        hg = sb("hg", [128, 2, FC, NTOK])
        pat_sb = hg[:, 0, :, :]
        dA = hg[:, 1, 0:RA, :]
        tokw_sb = sb("tokw_sb", [128, PC, D])
        tokb_sb = sb("tokb_sb", [128, D])
        sm_sb = sb("sm_sb", [128, LAYERS, C, SM])
        alog_sb = sb("alog_sb", [128, LAYERS, C, NST])
        acap_sb = sb("acap_sb", [128, LAYERS, C, NST])
        ea_sb = sb("ea_sb", [128, LAYERS, C, NST])
        na_sb = sb("na_sb", [128, LAYERS, C, NST])
        lngb_sb = sb("lngb_sb", [128, LAYERS, 2, D])
        inw_sb = sb("inw_sb", [DK, 2, 2 * DI])
        xpw_sb = sb("xpw_sb", [128, C, 128])
        dtw_sb = sb("dtw_sb", [RANK, DI])
        outw_sb = sb("outw_sb", [128, C, D])
        zeros = sb("zeros", [128, 512], bf16)
        h0 = sb("h0", [128, G, 2, D])
        xres = sb("xres", [128, G, 2, D])
        resb = sb("resb", [128, G, 2, D])
        xT = sb("xT", [DK, G, 2, GT])
        acc = sb("acc", [128, C, GT])
        xc = sb("xc", [128, G, C, GT])
        sz = sb("sz", [128, G, C, GT])
        dtlow = sb("dtlow", [RANK, GT])
        BC = sb("BC", [128, G, GT], bf16)
        rem = sb("rem", [128, GT])
        rem2 = sb("rem2", [128, GT])
        absx = sb("absx", [128, C, GT])
        xdt = sb("xdt", [128, C, GT])
        raw = sb("raw", [128, C + 1, GT])
        zexp = sb("zexp", [128, C, GT])
        lnw = sb("lnw", [128, C, GT])
        wm1 = sb("wm1", [128, C, GT])
        lp = sb("lp", [128, C, GT])
        dt = sb("dt", [128, G, C, GT])
        u = sb("u", [128, G, C, GT])
        hs = sb("hs", [128, RH, 2 * GT])
        hC = sb("hC", [128, RC, 2 * GT])
        Cb = sb("Cb", [128, RCB, 2 * GT])
        ys = sb("ys", [128, C, GT])
        yg = sb("yg", [128, C, GT])
        bst = sb("bst", [128, 2, 6])
        mv = sb("mv", [128, 2, 2])
        vpe = sb("vpe", [128, 2])
        mhalf = sb("mhalf", [128, TC])
        rstd = sb("rstd", [128, 2])
        nrm = sb("nrm", [128, 2, D])
        nrmg = sb("nrmg", [128, 2, D])

        iota_sb = sb("iota_sb", [128, E])
        wr_sb = sb("wr_sb", [DK, 2, E])
        bo_sb = sb("bo_sb", [E, D])
        bi_sb = sb("bi_sb", [128, E, FC])
        wi_sb = sb("wi_sb", [DK, 2, 2, F])
        wo_sb = sb("wo_sb", [128, 2, FC, D])
        hsum = sb("hsum", [128, TC, D])
        fst = sb("fst", [128, TC, 6])
        fmv = sb("fmv", [128, TC, 2])
        fvpe = sb("fvpe", [128, TC])
        frstd = sb("frstd", [128, TC])
        hh = sb("hh", [128, TC, D])
        hT = sb("hT", [DK, 2, NTOK])
        top = sb("top", [128, TC, 8])
        topi = sb("topi", [128, TC, 8], u32)
        topf = sb("topf", [128, TC, 8])
        gap = sb("gap", [128, TC])
        egap = sb("egap", [128, TC])
        den = sb("den", [128, TC])
        wtop = sb("wtop", [128, 2, TC])
        gw = sb("gw", [128, TC, E])
        gw2 = sb("gw2", [128, TC, E])
        gate = sb("gate", [128, TC, E])
        gateT = sb("gateT", [E, NTOK])
        facc = sb("facc", [128, TC, D])
        fout = sb("fout", [128, TC, D])

        psY = pb("psY", [128, 2, 512])
        psB = pb("psB", [128, 2, 512])
        psD = pb("psD", [128, 2, 512])
        psC = pb("psC", [128, 512])
        psS = pb("psS", [128, 512])

        def Y(c):
            return psY[:, c // 2, (c % 2) * GT:(c % 2 + 1) * GT]

        def half(i):
            return psS[:, i * GT:(i + 1) * GT]

        def bt(ap):
            return ap.rearrange("p (b t) -> p b t", t=T)

        ld_const, ld_tok, ld_sm = sem("ld_const"), sem("ld_tok"), sem("ld_sm")
        ld_pre, ld_post = sem("ld_pre"), sem("ld_post")
        zeros_set, dA_zero, mhalf_set, acap_done = sem("zeros_set"), sem("dA_zero"), sem("mhalf_set"), sem("acap_done")
        sel_done = sem("sel_done")
        ea_done, na_done = sem("ea_done"), sem("na_done")
        tok_mm, tok_done, h0_done = sem("tok_mm"), sem("tok_done"), sem("h0_done")
        xT_mm, xT_done = sem("xT_mm"), sem("xT_done")
        in_mm = sem("in_mm")
        conv0, conv1, conv2, conv3 = sem("conv0"), sem("conv1"), sem("conv2"), sem("conv3")
        z_done, xc_done = sem("z_done"), sem("xc_done")
        xp_mm, dtlow_done, bch = sem("xp_mm"), sem("dtlow_done"), sem("bch")
        rem_done, bcm, rem2_done, bcl = sem("rem_done"), sem("bcm"), sem("rem2_done"), sem("bcl")
        dt_mm, abs_done, xdt_done, raw_done = sem("dt_mm"), sem("abs_done"), sem("xdt_done"), sem("raw_done")
        zexp_done, lnw_done, wm1_done = sem("zexp_done"), sem("lnw_done"), sem("wm1_done")
        lpa, lpb, lpc = sem("lpa"), sem("lpb"), sem("lpc")
        dt_done, u_done = sem("dt_done"), sem("u_done")
        B_mm, C_mm, Cb_done = sem("B_mm"), sem("C_mm"), sem("Cb_done")
        dA_done, mul_done, scan_done, hC_done, y_mm = (sem("dA_done"), sem("mul_done"), sem("scan_done"),
                                                       sem("hC_done"), sem("y_mm"))
        y_zero = sem("y_zero")
        ys_done, yg_done, out_mm, bst_done, mv_done = (sem("ys_done"), sem("yg_done"), sem("out_mm"),
                                                       sem("bst_done"), sem("mv_done"))
        vpe_done, rstd_done, resb_done, nrm_done, nrmg_done, x_done = (
            sem("vpe_done"), sem("rstd_done"), sem("resb_done"), sem("nrm_done"), sem("nrmg_done"), sem("x_done"))
        out_done = sem("out_done")
        ld_ffn, ld_wi, ld_wo = sem("ld_ffn"), [sem("ld_wi0"), sem("ld_wi1")], [sem("ld_wo0"), sem("ld_wo1")]
        hsum_done, fst_done, fmv_done = sem("hsum_done"), sem("fst_done"), sem("fmv_done")
        fvpe_done, frstd_done, hh_done = sem("fvpe_done"), sem("frstd_done"), sem("hh_done")
        hT_mm, hT_done, logit_mm = sem("hT_mm"), sem("hT_done"), sem("logit_mm")
        top_done, topi_done, gap_done, egap_done = (sem("top_done"), sem("topi_done"), sem("gap_done"),
                                                    sem("egap_done"))
        topf_done, den_done, w1_done, w2_done = sem("topf_done"), sem("den_done"), sem("w1_done"), sem("w2_done")
        gw_done, gate_done, gateT_mm, gateT_done = (sem("gw_done"), sem("gate_done"), sem("gateT_mm"),
                                                    sem("gateT_done"))
        bo_mm, facc_done = sem("bo_mm"), sem("facc_done")
        up_mm, gelu_done, down_mm = sem("up_mm"), sem("gelu_done"), sem("down_mm")
        fin_done = sem("fin_done")
        LDPRE, LDPOST = 3 * 16, 1 * 16

        with nc.Block() as block:

            @block.sync
            def _(sp):
                sp.dma_start(tokw_sb[:, :, :], tok_w).then_inc(ld_tok, 16)
                for j in range(PC):
                    sp.dma_start(pat_sb[:, j, :], patches[:, j, :]).then_inc(ld_tok, 16)
                sp.dma_start(tokb_sb[:, :], tok_b).then_inc(ld_const, 16)
                sp.dma_start(ident[:, :], eye).then_inc(ld_const, 16)
                sp.dma_start(selc[:, :], sel).then_inc(ld_const, 16)
                sp.dma_start(sm_sb[:, :, :, :], smalls).then_inc(ld_sm, 16)
                sp.dma_start(alog_sb[:, :, :, :], a_log).then_inc(ld_sm, 16)
                sp.dma_start(lngb_sb[:, :, :, :], lngb).then_inc(ld_sm, 16)

                def load_pre(l):
                    if l:
                        sp.wait_ge(dt_mm, 2 * 2 * l)
                    sp.dma_start(inw_sb[:, :, :], in_w[l]).then_inc(ld_pre, 16)
                    sp.dma_start(xpw_sb[:, :, :], xp_w[l]).then_inc(ld_pre, 16)
                    sp.dma_start(dtw_sb[:, :], dt_w[l]).then_inc(ld_pre, 16)

                def load_post(l):
                    if l:
                        sp.wait_ge(out_mm, 2 * l)
                    sp.dma_start(outw_sb[:, :, :], out_w[l]).then_inc(ld_post, 16)

                load_pre(0)
                load_post(0)
                sp.dma_start(iota_sb[:, :], iota8).then_inc(ld_ffn, 16)
                sp.dma_start(wr_sb[:, :, :], wr).then_inc(ld_ffn, 16)
                sp.dma_start(bo_sb[:, :], bo).then_inc(ld_ffn, 16)
                sp.dma_start(bi_sb[:, :, :], bi).then_inc(ld_ffn, 16)
                for e in range(2):
                    sp.dma_start(wi_sb[:, e, :, :], wi[e]).then_inc(ld_wi[e], 16)
                    sp.dma_start(wo_sb[:, e, :, :], wo[e]).then_inc(ld_wo[e], 16)
                for l in range(1, LAYERS):
                    load_pre(l)
                    load_post(l)

            @block.tensor
            def _(pe):
                def tok(g):
                    if g:
                        pe.wait_ge(xT_done, g)
                    pe.wait_ge(ld_tok, 16 * (1 + PC))
                    for j in range(2):
                        lo = g * GT + j * 128
                        for k in range(PC):
                            mm = pe.matmul(psS[:, j * D:(j + 1) * D], pat_sb[:, k, lo:lo + 128], tokw_sb[:, k, :],
                                           start=(k == 0), stop=(k == PC - 1))
                    mm.then_inc(tok_mm, 1)

                def transposes(q, g):
                    pe.wait_ge(x_done, q + 1)
                    if q < 2:
                        pe.wait_ge(h0_done, q + 1)
                    for k in range(2):
                        for j in range(2):
                            mm = pe.transpose(psS[0:DK, k * GT + j * 128:k * GT + (j + 1) * 128],
                                              xres[:, g, j, k * DK:(k + 1) * DK], ident[:, :])
                    mm.then_inc(xT_mm, 1)

                def in_proj(g, e):
                    for h in range(2):
                        for k in range(2):
                            mm = pe.matmul(half(h), inw_sb[:, k, (e + h) * 128:(e + h + 1) * 128], xT[:, g, k, :],
                                           start=(k == 0), stop=(k == 1))
                    mm.then_inc(in_mm, 1)

                def pre_a(s, g, l):
                    pe.wait_ge(ld_pre, LDPRE * (l + 1))
                    pe.wait_ge(xT_done, s + 1)
                    in_proj(g, 0)

                def pre_b(s, g):
                    pe.wait_ge(raw_done, 2 * s + 1)
                    in_proj(g, 2)

                def pre_c(s, g):
                    pe.wait_ge(raw_done, 2 * s + 2)
                    in_proj(g, 4)

                def x_proj(s, g):
                    pe.wait_ge(xc_done, s + 1)
                    pe.wait_ge(z_done, s + 1)
                    for c in range(C):
                        mm = pe.matmul(half(0), xpw_sb[:, c, :], xc[:, g, c, :], start=(c == 0), stop=(c == C - 1))
                    mm.then_inc(xp_mm, 1)

                def dt_proj_a(s):
                    pe.wait_ge(dtlow_done, s + 1)
                    pe.wait_ge(rem_done, s + 1)
                    for c in range(2):
                        mm = pe.matmul(half(c), dtw_sb[:, c * 128:(c + 1) * 128], dtlow[:, :], start=True, stop=True)
                    mm.then_inc(dt_mm, 1)

                def dt_proj_b(s):
                    pe.wait_ge(xdt_done, C * s + 2)
                    pe.matmul(half(0), dtw_sb[:, 256:384], dtlow[:, :], start=True, stop=True).then_inc(dt_mm, 1)

                def out_proj(s, l):
                    pe.wait_ge(yg_done, s + 1)
                    pe.wait_ge(ld_post, LDPOST * (l + 1))
                    pe.wait_ge(xdt_done, C * min(s + 2, RUNS))
                    for j in range(2):
                        for c in range(C):
                            mm = pe.matmul(psS[:, j * D:(j + 1) * D], yg[:, c, j * 128:(j + 1) * 128], outw_sb[:, c, :],
                                           start=(c == 0), stop=(c == C - 1))
                    mm.then_inc(out_mm, 1)

                def broadcast(s, g, p):
                    n = PAIRS * s + p
                    if n == 0:
                        pe.wait_ge(sel_done, 1)
                    if p == 0:
                        pe.wait_ge(bcl, s + 1)
                    if n >= 2:
                        pe.wait_ge(mul_done, C * (n - 1))
                    for i in range(2):
                        mm = pe.matmul(psB[:, n % 2, i * GT:(i + 1) * GT], sel_sb[:, 2 * p + i, :], BC[:, g, :],
                                       start=True, stop=True)
                    mm.then_inc(B_mm, 1)
                    if n >= 1:
                        pe.wait_ge(Cb_done, n)
                    for i in range(2):
                        mm = pe.matmul(psC[:, i * GT:(i + 1) * GT], sel_sb[:, NST + 2 * p + i, :], BC[:, g, :],
                                       start=True, stop=True)
                    mm.then_inc(C_mm, 1)

                def y_clear(s):
                    if s:
                        pe.wait_ge(ys_done, C * s)
                    for i in range(2):
                        pe.matmul(psY[:, i, :], zeros[:, 0:128], zeros[:, :], start=True, stop=False,
                                  skip_group_check=True)

                def y_sum(s, k):
                    n = UNITS * s + k
                    pe.wait_ge(hC_done, n + 1)
                    for i in range(2):
                        mm = pe.matmul(Y(k % C), ident[:, :], hC[:, n % RC, i * GT:(i + 1) * GT],
                                       start=False, stop=(k >= UNITS - C and i == 1), skip_group_check=True)
                    mm.then_inc(y_mm, 1)

                pe.wait_ge(ld_const, 48)
                pe.wait_ge(zeros_set, 1)
                tok(0)
                transposes(0, 0)
                tok(1)
                transposes(1, 1)
                pe.wait_ge(xT_done, 2)
                pre_a(0, 0, 0)
                pre_b(0, 0)
                pre_c(0, 0)
                x_proj(0, 0)
                dt_proj_a(0)
                dt_proj_b(0)
                LAG = 3
                for s in range(RUNS):
                    l, g = s // 2, s % 2
                    for k in range(UNITS + LAG):
                        if k < UNITS:
                            if k == 0:
                                broadcast(s, g, 0)
                            if k % C == 0 and k // C + 1 < PAIRS:
                                broadcast(s, g, k // C + 1)
                        if k == LAG:
                            y_clear(s)
                        if k >= LAG:
                            y_sum(s, k - LAG)
                        if s > 0:
                            if k == 4:
                                out_proj(s - 1, (s - 1) // 2)
                            if k == 7 and s + 1 < RUNS:
                                transposes(s + 1, 1 - g)
                        if s + 1 < RUNS:
                            q = s + 1
                            if k == 8:
                                pre_a(q, 1 - g, q // 2)
                            if k == 11:
                                pre_b(q, 1 - g)
                            if k == 13:
                                pre_c(q, 1 - g)
                            if k == 15:
                                x_proj(q, 1 - g)
                            if k == 17:
                                dt_proj_a(q)
                            if k == 19:
                                dt_proj_b(q)
                out_proj(RUNS - 1, LAYERS - 1)

            @block.scalar
            def _(act):
                def xT_copy(q, g):
                    act.wait_ge(xT_mm, q + 1)
                    act.activation(xT[:, g, :, :], psS[0:DK, :].rearrange("p (k n) -> p k n", k=2),
                                   ACT.Copy).then_inc(xT_done, 1)

                def raw_copy(s, i):
                    act.wait_ge(in_mm, 3 * s + i + 1)
                    if s and i == 0:
                        act.wait_ge(conv3, C * s)
                        act.wait_ge(z_done, s)
                    act.activation(raw[:, 2 * i:2 * i + 2, :], psS[:, :].rearrange("p (i n) -> p i n", i=2),
                                   ACT.Copy).then_inc(raw_done, 1)

                def conv_last_tap(s, l, c):
                    act.wait_ge(raw_done, 2 * s + c // 2 + 1)
                    if c == 0 and s > 0:
                        act.wait_ge(xc_done, s)
                    act.activation(acc[:, c, :], raw[:, c, :], ACT.Identity,
                                   scale=sm_sb[:, l, c, SM_CONVW + 3:SM_CONVW + 4],
                                   bias=sm_sb[:, l, c, SM_CONVB:SM_CONVB + 1]).then_inc(conv0, 1)

                def silus(s, g):
                    act.wait_ge(conv3, C * (s + 1))
                    act.activation(xc[:, g, :, :], acc[:, :, :], ACT.Silu).then_inc(xc_done, 1)
                    act.activation(sz[:, g, 0, :], raw[:, C, :], ACT.Silu)
                    act.wait_ge(in_mm, 3 * s + 3)
                    act.activation(sz[:, g, 1:3, :], psS[:, :].rearrange("p (i n) -> p i n", i=2),
                                   ACT.Silu).then_inc(z_done, 1)

                def x_proj_out(s, g):
                    act.wait_ge(xp_mm, s + 1)
                    act.activation(dtlow[:, :], psS[0:RANK, 0:GT], ACT.Copy).then_inc(dtlow_done, 1)
                    act.activation(BC[:, g, :], half(0), ACT.Copy).then_inc(bch, 1)

                def dt_bias(s, l, c):
                    act.wait_ge(dt_mm, 2 * s + c // 2 + 1)
                    if c == 0 and s > 0:
                        act.wait_ge(dt_done, s)
                    act.activation(xdt[:, c, :], half(c % 2), ACT.Identity,
                                   bias=sm_sb[:, l, c, SM_DTB:SM_DTB + 1]).then_inc(xdt_done, 1)

                def softplus_exp(s):
                    act.wait_ge(xdt_done, C * (s + 1))
                    if s:
                        act.wait_ge(lpc, s)
                    act.activation(absx[:, :, :], xdt[:, :, :], ACT.Abs).then_inc(abs_done, 1)
                    act.wait_ge(abs_done, s + 1)
                    act.activation(zexp[:, :, :], absx[:, :, :], ACT.Exp, scale=-1.0).then_inc(zexp_done, 1)

                def softplus_ln(s):
                    act.wait_ge(zexp_done, s + 1)
                    act.activation(lnw[:, :, :], zexp[:, :, :], ACT.Ln, bias=1.0).then_inc(lnw_done, 1)

                def decay(s, l, g, k):
                    p, c = k // C, k % C
                    n = UNITS * s + k
                    if k == 0:
                        act.wait_ge(dt_done, s + 1)
                    if n >= RA:
                        act.wait_ge(scan_done, n - RA + 1)
                    for i in range(2):
                        st = 2 * p + i
                        a = act.activation(bt(dA[:, n % RA, i * GT:(i + 1) * GT])[:, :, 1:T],
                                           bt(dt[:, g, c, :])[:, :, 1:T], ACT.Exp,
                                           scale=na_sb[:, l, c, st:st + 1])
                    a.then_inc(dA_done, 1)

                def C_copy(s, p):
                    n = PAIRS * s + p
                    act.wait_ge(C_mm, n + 1)
                    if n >= RCB:
                        act.wait_ge(hC_done, C * (n - RCB + 1))
                    act.activation(Cb[:, n % RCB, :], psC[:, :], ACT.Copy).then_inc(Cb_done, 1)

                act.wait_ge(ld_const, 48)
                act.activation(sel_sb[:, :, :], selc[:, :].rearrange("p (n o) -> p n o", o=1)
                               .to_broadcast([128, 2 * NST, 128]), ACT.Copy).then_inc(sel_done, 1)
                act.wait_ge(ld_sm, 48)
                act.wait_ge(acap_done, 1)
                act.activation(ea_sb[:, :, :, :], acap_sb[:, :, :, :], ACT.Exp).then_inc(ea_done, 1)
                act.wait_ge(ea_done, 1)
                act.activation(na_sb[:, :, :, :], ea_sb[:, :, :, :], ACT.Copy, scale=-1.0).then_inc(na_done, 1)
                xT_copy(0, 0)
                xT_copy(1, 1)
                raw_copy(0, 0)
                raw_copy(0, 1)
                for c in range(C):
                    conv_last_tap(0, 0, c)
                silus(0, 0)
                x_proj_out(0, 0)
                for c in range(C):
                    dt_bias(0, 0, c)
                softplus_exp(0)
                softplus_ln(0)
                act.wait_ge(na_done, 1)
                act.wait_ge(dA_zero, 1)
                for s in range(RUNS):
                    l, g = s // 2, s % 2
                    q = s + 1
                    for k in range(UNITS):
                        if k == 0:
                            C_copy(s, 0)
                        decay(s, l, g, k)
                        if k % C == 1 and k // C + 1 < PAIRS:
                            C_copy(s, k // C + 1)
                        if q < RUNS:
                            ql, qg = q // 2, q % 2
                            if s > 0 and k == 8:
                                xT_copy(q, qg)
                            if k == 10:
                                raw_copy(q, 0)
                                conv_last_tap(q, ql, 0)
                                conv_last_tap(q, ql, 1)
                            if k == 12:
                                raw_copy(q, 1)
                                conv_last_tap(q, ql, 2)
                            if k == 14:
                                silus(q, qg)
                            if k == 16:
                                x_proj_out(q, qg)
                            if k == 18:
                                dt_bias(q, ql, 0)
                                dt_bias(q, ql, 1)
                            if k == 20:
                                dt_bias(q, ql, 2)
                            if k == 21:
                                softplus_exp(q)
                            if k == 22:
                                softplus_ln(q)

            @block.vector
            def _(dve):
                def tok_out(g):
                    dve.wait_ge(tok_mm, g + 1)
                    for dst, done in ((xres, x_done), (h0, h0_done)):
                        for j in range(2):
                            t = dve.tensor_tensor(dst[:, g, j, :], psS[:, j * D:(j + 1) * D], tokb_sb[:, :], ALU.add)
                        t.then_inc(done, 1)

                def conv_taps(s, l, cs):
                    sems = [conv1, conv2, conv3]
                    for k in range(1, KCONV):
                        for c in cs:
                            dve.wait_ge([conv0, conv1, conv2][k - 1], C * s + c + 1)
                            av = bt(acc[:, c, :])[:, :, k:T]
                            dve.scalar_tensor_tensor(av, bt(raw[:, c, :])[:, :, 0:T - k],
                                                     sm_sb[:, l, c, SM_CONVW + 3 - k:SM_CONVW + 4 - k], av,
                                                     ALU.mult, ALU.add).then_inc(sems[k - 1], 1)

                def split_bc(s, g):
                    dve.wait_ge(bch, s + 1)
                    dve.tensor_tensor(rem[:, :], half(0), BC[:, g, :], ALU.subtract).then_inc(rem_done, 1)

                def split_bc2(s, g):
                    dve.wait_ge(rem_done, s + 1)
                    dve.tensor_copy(BC[64:128, g, :], rem[64:128, :]).then_inc(bcm, 1)
                    dve.wait_ge(bcm, s + 1)
                    dve.tensor_tensor(rem2[96:128, :], rem[96:128, :], BC[96:128, g, :], ALU.subtract).then_inc(rem2_done, 1)
                    dve.wait_ge(rem2_done, s + 1)
                    dve.tensor_copy(BC[96:128, g, :], rem2[96:128, :]).then_inc(bcl, 1)

                def softplus_round(s):
                    dve.wait_ge(zexp_done, s + 1)
                    dve.tensor_scalar(wm1[:, :, :], zexp[:, :, :], 1.0, 1.0, ALU.add, ALU.subtract).then_inc(wm1_done, 1)

                def softplus_end(s, g):
                    dve.wait_ge(lpb, s + 1)
                    dve.scalar_tensor_tensor(lnw[:, :, :], zexp[:, :, :], 0.5, lp[:, :, :], ALU.mult,
                                             ALU.max).then_inc(lpc, 1)
                    dve.wait_ge(lpc, s + 1)
                    dve.scalar_tensor_tensor(dt[:, g, :, :], xdt[:, :, :], 0.0, lnw[:, :, :], ALU.max,
                                             ALU.add).then_inc(dt_done, 1)
                    dve.wait_ge(dt_done, s + 1)
                    dve.tensor_tensor(u[:, g, :, :], dt[:, g, :, :], xc[:, g, :, :], ALU.mult).then_inc(u_done, 1)

                def mul(s, g, k):
                    p, c = k // C, k % C
                    n = UNITS * s + k
                    if k == 0:
                        dve.wait_ge(u_done, s + 1)
                    if c == 0:
                        dve.wait_ge(B_mm, PAIRS * s + p + 1)
                    if n >= 2:
                        dve.wait_ge(scan_done, n - 1)
                    dve.tensor_tensor(psD[:, n % 2, :].rearrange("p (i n) -> p i n", i=2),
                                      u[:, g, c:c + 1, :].to_broadcast([128, 2, GT]),
                                      psB[:, (PAIRS * s + p) % 2, :].rearrange("p (i n) -> p i n", i=2),
                                      ALU.mult).then_inc(mul_done, 1)

                def scan(s, k):
                    n = UNITS * s + k
                    dve.wait_ge(dA_done, n + 1)
                    dve.wait_ge(mul_done, n + 1)
                    if n >= RH:
                        dve.wait_ge(hC_done, n - RH + 1)
                    dve.tensor_tensor_scan(hs[:, n % RH, :], dA[:, n % RA, :], psD[:, n % 2, :], 0.0,
                                           ALU.mult, ALU.add).then_inc(scan_done, 1)

                def gate_a(s, l, g):
                    dve.wait_ge(y_mm, UNITS * (s + 1))
                    for c in range(C):
                        dve.scalar_tensor_tensor(ys[:, c, :], xc[:, g, c, :], sm_sb[:, l, c, SM_DP:SM_DP + 1], Y(c),
                                                 ALU.mult, ALU.add).then_inc(ys_done, 1)

                def gate_b(s, g):
                    dve.wait_ge(ys_done, C * (s + 1))
                    if s:
                        dve.wait_ge(out_mm, s)
                    dve.tensor_tensor(yg[:, :, :], ys[:, :, :], sz[:, g, :, :], ALU.mult).then_inc(yg_done, 1)

                def norm_stats(s):
                    dve.wait_ge(out_mm, s + 1)
                    for j in range(2):
                        dve.bn_stats(bst[:, j, :], psS[:, j * D:(j + 1) * D]).then_inc(bst_done, 1)
                    for j in range(2):
                        dve.wait_ge(bst_done, 2 * s + 1 + j)
                        dve.bn_aggr(mv[:, j, :], bst[:, j, :]).then_inc(mv_done, 1)

                def norm_apply(s, l, g):
                    dve.wait_ge(rstd_done, s + 1)
                    for j in range(2):
                        dve.tensor_scalar(nrm[:, j, :], psS[:, j * D:(j + 1) * D], mv[:, j, 0:1], rstd[:, j:j + 1],
                                          ALU.subtract, ALU.mult).then_inc(nrm_done, 1)
                    dve.wait_ge(nrm_done, 2 * (s + 1))
                    dve.tensor_tensor(nrmg[:, :, :], nrm[:, :, :],
                                      lngb_sb[:, l, 0:1, :].to_broadcast([128, 2, D]), ALU.mult).then_inc(nrmg_done, 1)
                    dve.wait_ge(nrmg_done, s + 1)
                    dve.wait_ge(resb_done, s + 1)
                    dve.tensor_tensor(xres[:, g, :, :], nrmg[:, :, :], resb[:, g, :, :], ALU.add).then_inc(x_done, 1)

                dve.memset(zeros[:, :], 0.0).then_inc(zeros_set, 1)
                dve.memset(dA[:, :, :], 0.0).then_inc(dA_zero, 1)
                dve.wait_ge(ld_const, 48)
                dve.wait_ge(ld_sm, 48)
                dve.tensor_scalar(acap_sb[:, :, :, :], alog_sb[:, :, :, :], A_LOG_MAX, None,
                                  ALU.min).then_inc(acap_done, 1)
                tok_out(0)
                tok_out(1)
                conv_taps(0, 0, (0, 1))
                conv_taps(0, 0, (2,))
                split_bc(0, 0)
                split_bc2(0, 0)
                softplus_round(0)
                softplus_end(0, 0)
                for s in range(RUNS):
                    l, g = s // 2, s % 2
                    q = s + 1
                    ql, qg = q // 2, q % 2
                    mul(s, g, 0)
                    for k in range(UNITS):
                        if k + 1 < UNITS:
                            mul(s, g, k + 1)
                        scan(s, k)
                        if s > 0:
                            pl = (s - 1) // 2
                            if k == 2:
                                gate_a(s - 1, pl, 1 - g)
                            if k == 3:
                                gate_b(s - 1, 1 - g)
                            if k == 5:
                                norm_stats(s - 1)
                            if k == 6:
                                norm_apply(s - 1, pl, 1 - g)
                        if q < RUNS:
                            if k == 10:
                                conv_taps(q, ql, (0, 1))
                            if k == 12:
                                conv_taps(q, ql, (2,))
                            if k == 16:
                                split_bc(q, qg)
                            if k == 17:
                                split_bc2(q, qg)
                            if k == 21:
                                softplus_round(q)
                            if k == 23:
                                softplus_end(q, qg)
                s = RUNS - 1
                gate_a(s, LAYERS - 1, 1)
                gate_b(s, 1)
                norm_stats(s)
                norm_apply(s, LAYERS - 1, 1)

            @block.gpsimd
            def _(pool):
                pool.memset(mhalf[:, :], -0.5).then_inc(mhalf_set, 1)

                def res_bias(s, l, g):
                    pool.wait_ge(x_done, s + 1)
                    pool.tensor_tensor(resb[:, g, :, :], xres[:, g, :, :],
                                       lngb_sb[:, l, 1:2, :].to_broadcast([128, 2, D]), ALU.add).then_inc(resb_done, 1)

                def rstd_pow(s):
                    pool.wait_ge(mv_done, 2 * (s + 1))
                    if s:
                        pool.wait_ge(rstd_done, s)
                    pool.tensor_scalar(vpe[:, :], mv[:, :, 1], EPS, None, ALU.add).then_inc(vpe_done, 1)
                    pool.wait_ge(vpe_done, s + 1)
                    pool.tensor_tensor(rstd[:, :], vpe[:, :], mhalf[:, 0:2], ALU.pow).then_inc(rstd_done, 1)

                def log1p_a(s):
                    pool.wait_ge(wm1_done, s + 1)
                    pool.wait_ge(lnw_done, s + 1)
                    pool.tensor_tensor(lp[:, :, :], lnw[:, :, :], wm1[:, :, :], ALU.subtract).then_inc(lpa, 1)
                    pool.wait_ge(lpa, s + 1)
                    pool.tensor_tensor(lp[:, :, :], lp[:, :, :], zexp[:, :, :], ALU.add).then_inc(lpb, 1)

                def times_C(s, k):
                    p, c = k // C, k % C
                    n = UNITS * s + k
                    pool.wait_ge(scan_done, n + 1)
                    if c == 0:
                        pool.wait_ge(Cb_done, PAIRS * s + p + 1)
                    if n >= RC:
                        pool.wait_ge(y_mm, n - RC + 1)
                    pool.tensor_tensor(hC[:, n % RC, :], hs[:, n % RH, :], Cb[:, (PAIRS * s + p) % RCB, :],
                                       ALU.mult).then_inc(hC_done, 1)

                pool.wait_ge(mhalf_set, 1)
                pool.wait_ge(ld_sm, 48)
                log1p_a(0)
                for s in range(RUNS):
                    l, g = s // 2, s % 2
                    for k in range(UNITS):
                        times_C(s, k)
                        if k == 0:
                            res_bias(s, l, g)
                        if s > 0 and k == 4:
                            rstd_pow(s - 1)
                        if s + 1 < RUNS and k == 22:
                            log1p_a(s + 1)
                rstd_pow(RUNS - 1)

        up = [psY[:, 0, :], psY[:, 1, :], psB[:, 0, :], psB[:, 1, :]]
        RU = len(up)

        def down(j):
            return psD[:, j // 2, (j % 2) * D:(j % 2 + 1) * D]

        with nc.Block() as block:

            @block.sync
            def _(sp):
                for e in range(2, E):
                    sp.wait_ge(up_mm, FC * (e - 1))
                    sp.dma_start(wi_sb[:, e % 2, :, :], wi[e]).then_inc(ld_wi[e % 2], 16)
                    sp.wait_ge(down_mm, 2 * (e - 1))
                    sp.dma_start(wo_sb[:, e % 2, :, :], wo[e]).then_inc(ld_wo[e % 2], 16)
                sp.wait_ge(fin_done, TC)
                sp.dma_start(out.rearrange("(j p) d -> p j d", p=128), fout[:, :, :]).then_inc(out_done, 16)
                sp.wait_ge(out_done, 16)

            @block.tensor
            def _(pe):
                pe.wait_ge(hh_done, TC)
                for k in range(2):
                    for j in range(TC):
                        mm = pe.transpose(psB[0:DK, k, j * 128:(j + 1) * 128], hh[:, j, k * DK:(k + 1) * DK],
                                          ident[:, :])
                    mm.then_inc(hT_mm, 1)
                pe.wait_ge(hT_done, 2)
                pe.wait_ge(ld_ffn, 64)
                for j in range(TC):
                    for k in range(2):
                        mm = pe.matmul(psC[:, j * E:(j + 1) * E], hT[:, k, j * 128:(j + 1) * 128], wr_sb[:, k, :],
                                       start=(k == 0), stop=(k == 1))
                mm.then_inc(logit_mm, 1)

                def up_proj(e):
                    pe.wait_ge(ld_wi[e % 2], 16 * (e // 2 + 1))
                    for f in range(FC):
                        n = FC * e + f
                        if n >= RU:
                            pe.wait_ge(gelu_done, n - RU + 1)
                        for k in range(2):
                            mm = pe.matmul(up[n % RU], wi_sb[:, e % 2, k, f * 128:(f + 1) * 128], hT[:, k, :],
                                           start=(k == 0), stop=(k == 1))
                        mm.then_inc(up_mm, 1)

                def down_proj(e):
                    pe.wait_ge(ld_wo[e % 2], 16 * (e // 2 + 1))
                    pe.wait_ge(gelu_done, FC * (e + 1))
                    for j in range(TC):
                        if j % 2 == 0:
                            pe.wait_ge(facc_done, TC * e + j + 2)
                        for f in range(FC):
                            mm = pe.matmul(down(j), hg[:, e % 2, f, j * 128:(j + 1) * 128], wo_sb[:, e % 2, f, :],
                                           start=(f == 0), stop=(f == FC - 1))
                        if j % 2:
                            mm.then_inc(down_mm, 1)

                up_proj(0)
                pe.wait_ge(gate_done, 1)
                for j in range(TC):
                    mm = pe.transpose(psS[0:E, j * 128:(j + 1) * 128], gate[:, j, :], ident[:, :])
                mm.then_inc(gateT_mm, 1)
                pe.wait_ge(gateT_done, 1)
                for j in range(TC):
                    mm = pe.matmul(down(j), gateT[:, j * 128:(j + 1) * 128], bo_sb[:, :], start=True, stop=True)
                mm.then_inc(bo_mm, 1)
                for e in range(E):
                    if e + 1 < E:
                        up_proj(e + 1)
                    down_proj(e)

            @block.scalar
            def _(act):
                for k in range(2):
                    act.wait_ge(hT_mm, k + 1)
                    act.activation(hT[:, k, :], psB[0:DK, k, :], ACT.Copy).then_inc(hT_done, 1)
                act.wait_ge(gap_done, 1)
                act.activation(egap[:, :], gap[:, :], ACT.Exp).then_inc(egap_done, 1)

                def gelu(e):
                    for f in range(FC):
                        n = FC * e + f
                        act.wait_ge(up_mm, n + 1)
                        if e >= 2 and f == 0:
                            act.wait_ge(down_mm, 2 * (e - 1))
                        act.activation(hg[:, e % 2, f, :], up[n % RU], ACT.Gelu,
                                       bias=bi_sb[:, e, f:f + 1]).then_inc(gelu_done, 1)

                gelu(0)
                act.wait_ge(gateT_mm, 1)
                act.activation(gateT[:, :], psS[0:E, :], ACT.Copy).then_inc(gateT_done, 1)
                for e in range(1, E):
                    gelu(e)

            @block.vector
            def _(dve):
                def norm(i, src, dst, sums_done, done):
                    dve.wait_ge(sums_done[0], sums_done[1])
                    for j in range(TC):
                        dve.bn_stats(fst[:, j, :], src[:, j, :]).then_inc(fst_done, 1)
                    for j in range(TC):
                        dve.wait_ge(fst_done, TC * i + j + 1)
                        dve.bn_aggr(fmv[:, j, :], fst[:, j, :]).then_inc(fmv_done, 1)
                    dve.wait_ge(frstd_done, i + 1)
                    for j in range(TC):
                        dve.tensor_scalar(dst[:, j, :], src[:, j, :], fmv[:, j, 0:1], frstd[:, j:j + 1],
                                          ALU.subtract, ALU.mult).then_inc(done, 1)

                dve.wait_ge(x_done, RUNS + 2)
                dve.tensor_tensor(hsum[:, :, :], h0[:, :, :, :].rearrange("p g j d -> p (g j) d"),
                                  xres[:, :, :, :].rearrange("p g j d -> p (g j) d"), ALU.add).then_inc(hsum_done, 1)
                norm(0, hsum, hh, (hsum_done, 1), hh_done)

                dve.wait_ge(logit_mm, 1)
                for j in range(TC):
                    dve.max(top[:, j, :], psC[:, j * E:(j + 1) * E]).then_inc(top_done, 1)
                for j in range(TC):
                    dve.wait_ge(top_done, j + 1)
                    dve.max_index(topi[:, j, :], top[:, j, :], psC[:, j * E:(j + 1) * E]).then_inc(topi_done, 1)
                dve.tensor_tensor(gap[:, :], top[:, :, 1], top[:, :, 0], ALU.subtract).then_inc(gap_done, 1)
                dve.wait_ge(topi_done, TC)
                dve.tensor_copy(topf[:, :, :], topi[:, :, :]).then_inc(topf_done, 1)
                dve.wait_ge(egap_done, 1)
                dve.tensor_scalar(den[:, :], egap[:, :], 1.0, None, ALU.add).then_inc(den_done, 1)
                dve.wait_ge(den_done, 1)
                dve.reciprocal(wtop[:, 0, :], den[:, :]).then_inc(w1_done, 1)
                dve.wait_ge(w1_done, 1)
                dve.tensor_tensor(wtop[:, 1, :], egap[:, :], wtop[:, 0, :], ALU.mult).then_inc(w2_done, 1)
                dve.wait_ge(w2_done, 1)
                dve.wait_ge(topf_done, 1)
                dve.wait_ge(ld_ffn, 64)
                for i, dst in enumerate((gw, gw2)):
                    for j in range(TC):
                        dve.tensor_scalar(dst[:, j, :], iota_sb[:, :], topf[:, j, i:i + 1], wtop[:, i, j:j + 1],
                                          ALU.is_equal, ALU.mult).then_inc(gw_done, 1)
                dve.wait_ge(gw_done, 2 * TC)
                dve.tensor_tensor(gate[:, :, :], gw[:, :, :], gw2[:, :, :], ALU.add).then_inc(gate_done, 1)

                dve.wait_ge(bo_mm, 1)
                dve.wait_ge(hh_done, TC)
                for j in range(TC):
                    dve.tensor_tensor(facc[:, j, :], down(j), hh[:, j, :], ALU.add).then_inc(facc_done, 1)
                for e in range(E):
                    for j in range(TC):
                        dve.wait_ge(down_mm, 2 * e + j // 2 + 1)
                        dve.wait_ge(facc_done, TC * e + j + 1)
                        dve.scalar_tensor_tensor(facc[:, j, :], down(j), gate[:, j, e:e + 1], facc[:, j, :],
                                                 ALU.mult, ALU.add).then_inc(facc_done, 1)
                norm(1, facc, fout, (facc_done, TC * (E + 1)), fin_done)

            @block.gpsimd
            def _(pool):
                for i in range(2):
                    pool.wait_ge(fmv_done, TC * (i + 1))
                    pool.tensor_scalar(fvpe[:, :], fmv[:, :, 1], EPS, None, ALU.add).then_inc(fvpe_done, 1)
                    pool.wait_ge(fvpe_done, i + 1)
                    pool.tensor_tensor(frstd[:, :], fvpe[:, :], mhalf[:, :], ALU.pow).then_inc(frstd_done, 1)


_ORDER = ["patches", "tok_w", "tok_b", "in_w", "xp_w", "dt_w", "out_w", "lngb", "smalls", "a_log",
          "wr", "wi", "bi", "wo", "bo", "eye", "sel", "iota8"]


def kernel(**inputs):
    import numpy as _np
    import concourse.bacc as _bacc
    from concourse import mybir as _mybir
    from concourse.bass_utils import run_bass_kernel_spmd as _run

    def rows(m, k):
        m = m.reshape(m.shape[:-2] + (k, m.shape[-2] // k, m.shape[-1]))
        return _np.moveaxis(m, -3, -2)

    def on_all(m):
        return _np.repeat(m[None], 128, 0)

    i = {n: _np.asarray(v) for n, v in inputs.items()}
    at = {n[len("L0_attn_"):]: v for n, v in i.items() if n.startswith("L0_attn_")}
    ff = {n[len("L0_ffn_"):]: v for n, v in i.items() if n.startswith("L0_ffn_")}
    a = {}
    side = int(T ** 0.5)
    p = i["x"].shape[-1] // side
    pt = i["x"].reshape(B, 3, side, p, side, p).transpose(0, 2, 4, 3, 5, 1).reshape(NTOK, PATCH)
    a["patches"] = rows(pt.T, PC)
    a["tok_w"] = rows(i["L0_tok_W"].T, PC)
    a["tok_b"] = on_all(i["L0_tok_b"])
    a["in_w"] = rows(at["in_proj_w"].transpose(0, 2, 1), 2)
    xp = at["x_proj_w"]
    bc = xp[:, RANK:]
    pad = _np.zeros((LAYERS, 2 * NST - RANK, DI), xp.dtype)
    a["xp_w"] = rows(_np.concatenate([xp[:, :RANK], pad, bc, bc, bc], 1).transpose(0, 2, 1), C)
    a["dt_w"] = at["dt_proj_w"].transpose(0, 2, 1)
    a["out_w"] = rows(at["out_proj_w"].transpose(0, 2, 1), C)
    a["lngb"] = on_all(_np.stack([at["ln_g"], at["ln_b"]], 1))
    small = _np.concatenate([at["conv_w"], at["conv_b"][..., None], at["dt_proj_b"][..., None],
                             at["D_param"][..., None]], -1)
    a["smalls"] = small.reshape(LAYERS, C, 128, SM).transpose(2, 0, 1, 3)
    a["a_log"] = at["A_log"].reshape(LAYERS, C, 128, NST).transpose(2, 0, 1, 3)
    a["wr"] = rows(ff["Wr"].T, 2)
    a["wi"] = rows(ff["Wi"].transpose(0, 2, 1), 2)
    a["bi"] = ff["bi"].reshape(E, FC, 128).transpose(2, 0, 1)
    a["wo"] = rows(ff["Wo"].transpose(0, 2, 1), FC)
    a["bo"] = ff["bo"]
    a["iota8"] = on_all(_np.arange(E, dtype=_np.float32))
    a["eye"] = _np.eye(128, dtype=_np.float32)
    a["sel"] = _np.concatenate([_np.zeros((32, 32), _np.float32)] + 3 * [_np.eye(32, dtype=_np.float32)], 0)

    nc = _bacc.Bacc("TRN2", target_bir_lowering=False, num_devices=1)
    arrays, args = {}, []
    for n in _ORDER:
        arrays[f"in_{n}_dram"] = _np.ascontiguousarray(a[n])
        args.append(nc.dram_tensor(f"in_{n}_dram", a[n].shape, _mybir.dt.from_np(a[n].dtype),
                                   kind="ExternalInput").ap())
    args.append(nc.dram_tensor("out_0_dram", (NTOK, D), _mybir.dt.float32, kind="ExternalOutput").ap())
    tower_program(nc, *args)
    r = _run(nc, [arrays], core_ids=[0])
    return r.results[0]["out_0_dram"].reshape(B, T, D)
```

```python
import concourse.bass as bass
from concourse import mybir
from contextlib import ExitStack

LAYERS = 4
D = 192
DI = 384
NST = 16
RANK = 12
KCONV = 4
T = 16
B = 32
G = 2
GB = B // G
GT = GB * T
NTOK = B * T
C = DI // 128
DK = D // 2
PATCH = 768
PC = PATCH // 128
EPS = 1e-5
A_LOG_MAX = 80.0
PAIRS = NST // 2
UNITS = PAIRS * C
RUNS = LAYERS * G
LAG = 5
AT_PE = dict(out_proj=3, transposes=8, pre_a=8, pre_b=9, pre_c=10, x_proj=12, dt_proj_a=15, dt_proj_b=16)
AT_ACT = dict(xT_copy=9, raw_a=10, raw_b=11, raw_c=12, silus=13, x_proj_out=14, dt_bias_a=17, dt_bias_b=18,
              exp=19, ln=22)
AT_DVE = dict(gate=0, stats=4, norm=5, conv_a=10, conv_b=12, split_a=14, split_b=14, round=19, floor=22,
              end=23)
AT_POOL = dict(res_bias=0, rstd=2, rest=18)
E = 8
F = 768
FC = F // 128
TC = NTOK // 128
SM_CONVW, SM_CONVB, SM_DTB, SM_DP = 0, 4, 5, 6
SM = 7


def tower_program(nc, patches, tok_w, tok_b, in_w, xp_w, dt_w, out_w, lngb, smalls, a_log,
                  wr, wi, bi, wo, bo, eye, sel, iota8, out):
    fp32 = mybir.dt.float32
    bf16 = mybir.dt.bfloat16
    u32 = mybir.dt.uint32
    fp32r = mybir.dt.float32r
    ALU = mybir.AluOpType
    ACT = mybir.ActivationFunctionType

    RA, RH, RC, RCB = 6, 4, 4, 3

    ctx = ExitStack()
    with ctx:
        stack_ctx = ExitStack()

        def sb(name, shape, dt=fp32):
            return ctx.enter_context(nc.sbuf_tensor(name, shape, dt))

        def sbs(name, shape, dt=fp32):
            return stack_ctx.enter_context(nc.sbuf_tensor(name, shape, dt))

        def pb(name, shape, dt=fp32):
            return ctx.enter_context(nc.psum_tensor(name, shape, dt))

        def sem(name):
            return ctx.enter_context(nc.semaphore(name))

        ident = sb("ident", [128, 128])
        zeros = sb("zeros", [128, 512], bf16)
        mhalf = sb("mhalf", [128, TC])
        h0 = sb("h0", [128, G, 2, D])
        xres = sb("xres", [128, G, 2, D])
        iota_sb = sb("iota_sb", [128, E])
        wr_sb = sb("wr_sb", [DK, 2, E])
        bo_sb = sb("bo_sb", [E, D])
        bi_sb = sb("bi_sb", [128, E, FC])
        wi_sb = sb("wi_sb", [DK, 2, 2, F])
        wo_sb = sb("wo_sb", [128, 2, FC, D])

        selc = sbs("selc", [128, 2 * NST])
        sel_sb = sbs("sel_sb", [128, 2 * NST, 128], bf16)
        pat_sb = sbs("pat_sb", [128, PC, NTOK])
        tokw_sb = sbs("tokw_sb", [128, PC, D])
        tokb_sb = sbs("tokb_sb", [128, D])
        sm_sb = sbs("sm_sb", [128, LAYERS, C, SM])
        alog_sb = sbs("alog_sb", [128, LAYERS, C, NST])
        acap_sb = sbs("acap_sb", [128, LAYERS, C, NST])
        ea_sb = sbs("ea_sb", [128, LAYERS, C, NST])
        na_sb = sbs("na_sb", [128, LAYERS, C, NST])
        lngb_sb = sbs("lngb_sb", [128, LAYERS, 2, D])
        inw_sb = sbs("inw_sb", [DK, 2, 2 * DI])
        xpw_sb = sbs("xpw_sb", [128, C, 128])
        dtw_sb = sbs("dtw_sb", [RANK, DI])
        outw_sb = sbs("outw_sb", [128, C, D])
        resb = sbs("resb", [128, G, 2, D])
        xT = sbs("xT", [DK, G, 2, GT])
        raw = sbs("raw", [128, 2 * C, GT])
        acc = sbs("acc", [128, C, GT])
        xc = sbs("xc", [128, G, C, GT])
        sz = sbs("sz", [128, G, C, GT])
        dtlow = sbs("dtlow", [RANK, GT])
        BC = sbs("BC", [128, G, GT], bf16)
        rem = sbs("rem", [128, GT])
        rem2 = sbs("rem2", [128, GT])
        xdt = sbs("xdt", [128, C, GT])
        absx = sbs("absx", [128, C, GT])
        zexp = sbs("zexp", [128, C, GT])
        lnw = sbs("lnw", [128, C, GT])
        wm1 = sbs("wm1", [128, C, GT])
        lp = sbs("lp", [128, C, GT])
        relx = sbs("relx", [128, C, GT])
        floor = sbs("floor", [128, C, GT])
        rest = sbs("rest", [128, C, GT])
        dt = sbs("dt", [128, G, C, GT])
        u = sbs("u", [128, G, C, GT])
        dA = sbs("dA", [128, RA, 2 * GT])
        hs = sbs("hs", [128, RH, 2 * GT])
        hC = sbs("hC", [128, RC, 2 * GT])
        Cb = sbs("Cb", [128, RCB, 2 * GT])
        ys = sbs("ys", [128, C, GT])
        yg = sbs("yg", [128, C, GT])
        bst = sbs("bst", [128, 2, 6])
        mv = sbs("mv", [128, 2, 2])
        vpe = sbs("vpe", [128, 2])
        rstd = sbs("rstd", [128, 2])
        nrm = sbs("nrm", [128, 2, D])
        nrmg = sbs("nrmg", [128, 2, D])

        psY = pb("psY", [128, 2, 512])
        psB = pb("psB", [128, 2, 512])
        psD = pb("psD", [128, 2, 512])
        psC = pb("psC", [128, 512])
        psS = pb("psS", [128, 512])

        def Y(c):
            return psY[:, c // 2, (c % 2) * GT:(c % 2 + 1) * GT]

        def half(i):
            return psS[:, i * GT:(i + 1) * GT]

        def bt(ap):
            return ap.rearrange("p (b t) -> p b t", t=T)

        ld_const, ld_tok, ld_sm = sem("ld_const"), [sem("ld_tok0"), sem("ld_tok1")], sem("ld_sm")
        ld_pre, ld_post = sem("ld_pre"), sem("ld_post")
        zeros_set, dA_zero, mhalf_set, acap_done = sem("zeros_set"), sem("dA_zero"), sem("mhalf_set"), sem("acap_done")
        sel_done = sem("sel_done")
        ea_done, na_done = sem("ea_done"), sem("na_done")
        tok_mm, tok_done, h0_done = sem("tok_mm"), sem("tok_done"), sem("h0_done")
        xT_mm, xT_done = sem("xT_mm"), sem("xT_done")
        in_mm = sem("in_mm")
        conv0, conv1, conv2, conv3 = sem("conv0"), sem("conv1"), sem("conv2"), sem("conv3")
        z_done, xc_done = sem("z_done"), sem("xc_done")
        xp_mm, dtlow_done, bch = sem("xp_mm"), sem("dtlow_done"), sem("bch")
        rem_done, bcm, rem2_done, bcl = sem("rem_done"), sem("bcm"), sem("rem2_done"), sem("bcl")
        dt_mm, abs_done, xdt_done, raw_done = sem("dt_mm"), sem("abs_done"), sem("xdt_done"), sem("raw_done")
        zexp_done, lnw_done, wm1_done = sem("zexp_done"), sem("lnw_done"), sem("wm1_done")
        lpa, lpb, relx_done, floor_done, rest_done = (sem("lpa"), sem("lpb"), sem("relx_done"), sem("floor_done"),
                                                      sem("rest_done"))
        dt_done, u_done = sem("dt_done"), sem("u_done")
        B_mm, C_mm, Cb_done = sem("B_mm"), sem("C_mm"), sem("Cb_done")
        dA_done, mul_done, scan_done, hC_done, y_mm = (sem("dA_done"), sem("mul_done"), sem("scan_done"),
                                                       sem("hC_done"), sem("y_mm"))
        y_zero = sem("y_zero")
        ys_done, yg_done, out_mm, bst_done, mv_done = (sem("ys_done"), sem("yg_done"), sem("out_mm"),
                                                       sem("bst_done"), sem("mv_done"))
        vpe_done, rstd_done, resb_done, nrm_done, nrmg_done, x_done = (
            sem("vpe_done"), sem("rstd_done"), sem("resb_done"), sem("nrm_done"), sem("nrmg_done"), sem("x_done"))
        out_done = sem("out_done")
        ld_ffn, ld_wi, ld_wo = sem("ld_ffn"), [sem("ld_wi0"), sem("ld_wi1")], [sem("ld_wo0"), sem("ld_wo1")]
        hsum_done, fst_done, fmv_done = sem("hsum_done"), sem("fst_done"), sem("fmv_done")
        fvpe_done, frstd_done, hh_done = sem("fvpe_done"), sem("frstd_done"), sem("hh_done")
        hT_mm, hT_done, logit_mm = sem("hT_mm"), sem("hT_done"), sem("logit_mm")
        top_done, topi_done, gap_done, egap_done = (sem("top_done"), sem("topi_done"), sem("gap_done"),
                                                    sem("egap_done"))
        topf_done, den_done, w1_done, w2_done = sem("topf_done"), sem("den_done"), sem("w1_done"), sem("w2_done")
        gw_done, gate_done, gateT_mm, gateT_done = (sem("gw_done"), sem("gate_done"), sem("gateT_mm"),
                                                    sem("gateT_done"))
        bo_mm, facc_done = sem("bo_mm"), sem("facc_done")
        up_mm, gelu_done, down_mm = sem("up_mm"), sem("gelu_done"), sem("down_mm")
        fin_done = sem("fin_done")
        wi_split, wo_split, hT_split, hghi_done, hg_split = (sem("wi_split"), sem("wo_split"), sem("hT_split"),
                                                             sem("hghi_done"), sem("hg_split"))
        LDPRE, LDPOST = 3 * 16, 1 * 16

        with nc.Block() as block:

            @block.sync
            def _(sp):
                sp.dma_start(tokw_sb[:, :, :], tok_w).then_inc(ld_tok[0], 16)
                for j in range(PC):
                    sp.dma_start(pat_sb[:, j, 0:GT], patches[:, j, 0:GT]).then_inc(ld_tok[0], 16)
                sp.dma_start(tokb_sb[:, :], tok_b).then_inc(ld_const, 16)
                sp.dma_start(ident[:, :], eye).then_inc(ld_const, 16)
                sp.dma_start(selc[:, :], sel).then_inc(ld_const, 16)
                sp.dma_start(sm_sb[:, :, :, :], smalls).then_inc(ld_sm, 16)
                sp.dma_start(alog_sb[:, :, :, :], a_log).then_inc(ld_sm, 16)
                sp.dma_start(lngb_sb[:, :, :, :], lngb).then_inc(ld_sm, 16)

                def load_pre(l):
                    if l:
                        sp.wait_ge(dt_mm, 2 * 2 * l)
                    sp.dma_start(inw_sb[:, :, :], in_w[l]).then_inc(ld_pre, 16)
                    sp.dma_start(xpw_sb[:, :, :], xp_w[l]).then_inc(ld_pre, 16)
                    sp.dma_start(dtw_sb[:, :], dt_w[l]).then_inc(ld_pre, 16)

                def load_post(l):
                    if l:
                        sp.wait_ge(out_mm, 2 * l)
                    sp.dma_start(outw_sb[:, :, :], out_w[l]).then_inc(ld_post, 16)

                load_pre(0)
                for j in range(PC):
                    sp.dma_start(pat_sb[:, j, GT:], patches[:, j, GT:]).then_inc(ld_tok[1], 16)
                load_post(0)
                sp.dma_start(iota_sb[:, :], iota8).then_inc(ld_ffn, 16)
                sp.dma_start(wr_sb[:, :, :], wr).then_inc(ld_ffn, 16)
                sp.dma_start(bo_sb[:, :], bo).then_inc(ld_ffn, 16)
                sp.dma_start(bi_sb[:, :, :], bi).then_inc(ld_ffn, 16)
                for e in range(2):
                    sp.dma_start(wi_sb[:, e, :, :], wi[e]).then_inc(ld_wi[e], 16)
                    sp.dma_start(wo_sb[:, e, :, :], wo[e]).then_inc(ld_wo[e], 16)
                for l in range(1, LAYERS):
                    load_pre(l)
                    load_post(l)

            @block.tensor
            def _(pe):
                def tok(g):
                    if g:
                        pe.wait_ge(xdt_done, C)
                    pe.wait_ge(ld_tok[g], 16 * (1 + PC) if g == 0 else 16 * PC)
                    for j in range(2):
                        lo = g * GT + j * 128
                        for k in range(PC):
                            mm = pe.matmul(psS[:, j * D:(j + 1) * D], pat_sb[:, k, lo:lo + 128], tokw_sb[:, k, :],
                                           start=(k == 0), stop=(k == PC - 1))
                    mm.then_inc(tok_mm, 1)

                def transposes(q, g):
                    pe.wait_ge(x_done, q + 1)
                    if q < 2:
                        pe.wait_ge(h0_done, q + 1)
                    for k in range(2):
                        for j in range(2):
                            mm = pe.transpose(psS[0:DK, k * GT + j * 128:k * GT + (j + 1) * 128],
                                              xres[:, g, j, k * DK:(k + 1) * DK], ident[:, :])
                    mm.then_inc(xT_mm, 1)

                def in_proj(g, e):
                    for h in range(2):
                        for k in range(2):
                            mm = pe.matmul(half(h), inw_sb[:, k, (e + h) * 128:(e + h + 1) * 128], xT[:, g, k, :],
                                           start=(k == 0), stop=(k == 1))
                    mm.then_inc(in_mm, 1)

                def pre_a(s, g, l):
                    pe.wait_ge(ld_pre, LDPRE * (l + 1))
                    pe.wait_ge(xT_done, s + 1)
                    in_proj(g, 0)

                def pre_b(s, g):
                    pe.wait_ge(raw_done, C * s + 1)
                    in_proj(g, 2)

                def pre_c(s, g):
                    pe.wait_ge(raw_done, C * s + 2)
                    in_proj(g, 4)

                def x_proj(s, g):
                    pe.wait_ge(xc_done, s + 1)
                    pe.wait_ge(raw_done, C * (s + 1))
                    for c in range(C):
                        mm = pe.matmul(half(0), xpw_sb[:, c, :], xc[:, g, c, :], start=(c == 0), stop=(c == C - 1))
                    mm.then_inc(xp_mm, 1)

                def dt_proj_a(s):
                    pe.wait_ge(dtlow_done, s + 1)
                    pe.wait_ge(rem_done, s + 1)
                    for c in range(2):
                        mm = pe.matmul(half(c), dtw_sb[:, c * 128:(c + 1) * 128], dtlow[:, :], start=True, stop=True)
                    mm.then_inc(dt_mm, 1)

                def dt_proj_b(s):
                    pe.wait_ge(xdt_done, C * s + 2)
                    pe.matmul(half(0), dtw_sb[:, 256:384], dtlow[:, :], start=True, stop=True).then_inc(dt_mm, 1)

                def out_proj(s, l):
                    pe.wait_ge(yg_done, s + 1)
                    pe.wait_ge(ld_post, LDPOST * (l + 1))
                    pe.wait_ge(xdt_done, C * min(s + 2, RUNS))
                    for j in range(2):
                        for c in range(C):
                            mm = pe.matmul(psS[:, j * D:(j + 1) * D], yg[:, c, j * 128:(j + 1) * 128], outw_sb[:, c, :],
                                           start=(c == 0), stop=(c == C - 1))
                    mm.then_inc(out_mm, 1)

                def broadcast(s, g, p):
                    n = PAIRS * s + p
                    if n == 0:
                        pe.wait_ge(sel_done, 1)
                    if p == 0:
                        pe.wait_ge(bcl, s + 1)
                    if n >= 2:
                        pe.wait_ge(mul_done, C * (n - 1))
                    for i in range(2):
                        mm = pe.matmul(psB[:, n % 2, i * GT:(i + 1) * GT], sel_sb[:, 2 * p + i, :], BC[:, g, :],
                                       start=True, stop=True)
                    mm.then_inc(B_mm, 1)
                    if n >= 1:
                        pe.wait_ge(Cb_done, n)
                    for i in range(2):
                        mm = pe.matmul(psC[:, i * GT:(i + 1) * GT], sel_sb[:, NST + 2 * p + i, :], BC[:, g, :],
                                       start=True, stop=True)
                    mm.then_inc(C_mm, 1)

                def y_clear(s):
                    if s:
                        pe.wait_ge(ys_done, C * s)
                    for i in range(2):
                        pe.matmul(psY[:, i, :], zeros[:, 0:128], zeros[:, :], start=True, stop=False,
                                  skip_group_check=True)

                def y_sum(s, k):
                    n = UNITS * s + k
                    pe.wait_ge(hC_done, n + 1)
                    for i in range(2):
                        mm = pe.matmul(Y(k % C), ident[:, :], hC[:, n % RC, i * GT:(i + 1) * GT],
                                       start=False, stop=(k >= UNITS - C and i == 1), skip_group_check=True)
                    mm.then_inc(y_mm, 1)

                pe.wait_ge(ld_const, 48)
                pe.wait_ge(zeros_set, 1)
                tok(0)
                transposes(0, 0)
                pre_a(0, 0, 0)
                pre_b(0, 0)
                pre_c(0, 0)
                x_proj(0, 0)
                dt_proj_a(0)
                dt_proj_b(0)
                tok(1)
                transposes(1, 1)
                for s in range(RUNS):
                    l, g = s // 2, s % 2
                    for k in range(UNITS + LAG):
                        if k < UNITS:
                            if k == 0:
                                broadcast(s, g, 0)
                            if k % C == 0 and k // C + 1 < PAIRS:
                                broadcast(s, g, k // C + 1)
                        if k == LAG:
                            y_clear(s)
                        if k >= LAG:
                            y_sum(s, k - LAG)
                        if s > 0:
                            if k == AT_PE['out_proj']:
                                out_proj(s - 1, (s - 1) // 2)
                            if k == AT_PE['transposes'] and s + 1 < RUNS:
                                transposes(s + 1, 1 - g)
                        if s + 1 < RUNS:
                            q = s + 1
                            if k == AT_PE['pre_a']:
                                pre_a(q, 1 - g, q // 2)
                            if k == AT_PE['pre_b']:
                                pre_b(q, 1 - g)
                            if k == AT_PE['pre_c']:
                                pre_c(q, 1 - g)
                            if k == AT_PE['x_proj']:
                                x_proj(q, 1 - g)
                            if k == AT_PE['dt_proj_a']:
                                dt_proj_a(q)
                            if k == AT_PE['dt_proj_b']:
                                dt_proj_b(q)
                out_proj(RUNS - 1, LAYERS - 1)

            @block.scalar
            def _(act):
                def xT_copy(q, g):
                    act.wait_ge(xT_mm, q + 1)
                    act.activation(xT[:, g, :, :], psS[0:DK, :].rearrange("p (k n) -> p k n", k=2),
                                   ACT.Copy).then_inc(xT_done, 1)

                def raw_copy(s, i):
                    act.wait_ge(in_mm, C * s + i + 1)
                    if s and i == 0:
                        act.wait_ge(conv3, C * s)
                        act.wait_ge(z_done, s)
                    act.activation(raw[:, 2 * i:2 * i + 2, :], psS[:, :].rearrange("p (i n) -> p i n", i=2),
                                   ACT.Copy).then_inc(raw_done, 1)

                def conv_last_tap(s, l, c):
                    act.wait_ge(raw_done, C * s + c // 2 + 1)
                    if c == 0 and s > 0:
                        act.wait_ge(xc_done, s)
                    act.activation(acc[:, c, :], raw[:, c, :], ACT.Identity,
                                   scale=sm_sb[:, l, c, SM_CONVW + 3:SM_CONVW + 4],
                                   bias=sm_sb[:, l, c, SM_CONVB:SM_CONVB + 1]).then_inc(conv0, 1)

                def silus(s, g):
                    act.wait_ge(conv3, C * (s + 1))
                    act.activation(xc[:, g, :, :], acc[:, :, :], ACT.Silu).then_inc(xc_done, 1)
                    act.wait_ge(raw_done, C * (s + 1))
                    act.activation(sz[:, g, :, :], raw[:, C:2 * C, :], ACT.Silu).then_inc(z_done, 1)

                def x_proj_out(s, g):
                    act.wait_ge(xp_mm, s + 1)
                    act.activation(dtlow[:, :], psS[0:RANK, 0:GT], ACT.Copy).then_inc(dtlow_done, 1)
                    act.activation(BC[:, g, :], half(0), ACT.Copy).then_inc(bch, 1)

                def dt_bias(s, l, c):
                    act.wait_ge(dt_mm, 2 * s + c // 2 + 1)
                    if c == 0 and s > 0:
                        act.wait_ge(relx_done, s)
                    act.activation(xdt[:, c, :], half(c % 2), ACT.Identity,
                                   bias=sm_sb[:, l, c, SM_DTB:SM_DTB + 1]).then_inc(xdt_done, 1)

                def softplus_exp(s):
                    act.wait_ge(xdt_done, C * (s + 1))
                    if s:
                        act.wait_ge(floor_done, s)
                        act.wait_ge(rest_done, s)
                    act.activation(absx[:, :, :], xdt[:, :, :], ACT.Abs).then_inc(abs_done, 1)
                    act.wait_ge(abs_done, s + 1)
                    act.activation(zexp[:, :, :], absx[:, :, :], ACT.Exp, scale=-1.0).then_inc(zexp_done, 1)

                def softplus_ln(s):
                    act.wait_ge(zexp_done, s + 1)
                    if s:
                        act.wait_ge(lpb, s)
                    act.activation(lnw[:, :, :], zexp[:, :, :], ACT.Ln, bias=1.0).then_inc(lnw_done, 1)

                def decay(s, l, g, k):
                    p, c = k // C, k % C
                    n = UNITS * s + k
                    if k == 0:
                        act.wait_ge(dt_done, s + 1)
                    if n >= RA:
                        act.wait_ge(scan_done, n - RA + 1)
                    for i in range(2):
                        st = 2 * p + i
                        a = act.activation(bt(dA[:, n % RA, i * GT:(i + 1) * GT])[:, :, 1:T],
                                           bt(dt[:, g, c, :])[:, :, 1:T], ACT.Exp,
                                           scale=na_sb[:, l, c, st:st + 1])
                    a.then_inc(dA_done, 1)

                def C_copy(s, p):
                    n = PAIRS * s + p
                    act.wait_ge(C_mm, n + 1)
                    if n >= RCB:
                        act.wait_ge(hC_done, C * (n - RCB + 1))
                    act.activation(Cb[:, n % RCB, :], psC[:, :], ACT.Copy).then_inc(Cb_done, 1)

                act.wait_ge(ld_const, 48)
                act.activation(sel_sb[:, :, :], selc[:, :].rearrange("p (n o) -> p n o", o=1)
                               .to_broadcast([128, 2 * NST, 128]), ACT.Copy).then_inc(sel_done, 1)
                act.wait_ge(ld_sm, 48)
                act.wait_ge(acap_done, 1)
                act.activation(ea_sb[:, :, :, :], acap_sb[:, :, :, :], ACT.Exp).then_inc(ea_done, 1)
                act.wait_ge(ea_done, 1)
                act.activation(na_sb[:, :, :, :], ea_sb[:, :, :, :], ACT.Copy, scale=-1.0).then_inc(na_done, 1)
                xT_copy(0, 0)
                raw_copy(0, 0)
                raw_copy(0, 1)
                raw_copy(0, 2)
                for c in range(C):
                    conv_last_tap(0, 0, c)
                silus(0, 0)
                x_proj_out(0, 0)
                for c in range(C):
                    dt_bias(0, 0, c)
                softplus_exp(0)
                softplus_ln(0)
                xT_copy(1, 1)
                act.wait_ge(na_done, 1)
                act.wait_ge(dA_zero, 1)
                for s in range(RUNS):
                    l, g = s // 2, s % 2
                    q = s + 1
                    for k in range(UNITS):
                        if k == 0:
                            C_copy(s, 0)
                        decay(s, l, g, k)
                        if k % C == 1 and k // C + 1 < PAIRS:
                            C_copy(s, k // C + 1)
                        if q < RUNS:
                            ql, qg = q // 2, q % 2
                            if s > 0 and k == AT_ACT['xT_copy']:
                                xT_copy(q, qg)
                            if k == AT_ACT['raw_a']:
                                raw_copy(q, 0)
                                conv_last_tap(q, ql, 0)
                                conv_last_tap(q, ql, 1)
                            if k == AT_ACT['raw_b']:
                                raw_copy(q, 1)
                                conv_last_tap(q, ql, 2)
                            if k == AT_ACT['raw_c']:
                                raw_copy(q, 2)
                            if k == AT_ACT['silus']:
                                silus(q, qg)
                            if k == AT_ACT['x_proj_out']:
                                x_proj_out(q, qg)
                            if k == AT_ACT['dt_bias_a']:
                                dt_bias(q, ql, 0)
                                dt_bias(q, ql, 1)
                            if k == AT_ACT['dt_bias_b']:
                                dt_bias(q, ql, 2)
                            if k == AT_ACT['exp']:
                                softplus_exp(q)
                            if k == AT_ACT['ln']:
                                softplus_ln(q)

            @block.vector
            def _(dve):
                def tok_out(g):
                    dve.wait_ge(tok_mm, g + 1)
                    for dst, done in ((xres, x_done), (h0, h0_done)):
                        for j in range(2):
                            t = dve.tensor_tensor(dst[:, g, j, :], psS[:, j * D:(j + 1) * D], tokb_sb[:, :], ALU.add)
                        t.then_inc(done, 1)

                def conv_taps(s, l, cs):
                    sems = [conv1, conv2, conv3]
                    for k in range(1, KCONV):
                        for c in cs:
                            dve.wait_ge([conv0, conv1, conv2][k - 1], C * s + c + 1)
                            av = bt(acc[:, c, :])[:, :, k:T]
                            dve.scalar_tensor_tensor(av, bt(raw[:, c, :])[:, :, 0:T - k],
                                                     sm_sb[:, l, c, SM_CONVW + 3 - k:SM_CONVW + 4 - k], av,
                                                     ALU.mult, ALU.add).then_inc(sems[k - 1], 1)

                def split_bc(s, g):
                    dve.wait_ge(bch, s + 1)
                    dve.tensor_tensor(rem[:, :], half(0), BC[:, g, :], ALU.subtract).then_inc(rem_done, 1)

                def split_bc2(s, g):
                    dve.wait_ge(rem_done, s + 1)
                    dve.tensor_copy(BC[64:128, g, :], rem[64:128, :]).then_inc(bcm, 1)
                    dve.wait_ge(bcm, s + 1)
                    dve.tensor_tensor(rem2[96:128, :], rem[96:128, :], BC[96:128, g, :], ALU.subtract).then_inc(rem2_done, 1)
                    dve.wait_ge(rem2_done, s + 1)
                    dve.tensor_copy(BC[96:128, g, :], rem2[96:128, :]).then_inc(bcl, 1)

                def softplus_round(s):
                    dve.wait_ge(zexp_done, s + 1)
                    dve.tensor_scalar(wm1[:, :, :], zexp[:, :, :], 1.0, 1.0, ALU.add, ALU.subtract).then_inc(wm1_done, 1)

                def softplus_floor(s):
                    if s:
                        dve.wait_ge(dt_done, s)
                    dve.tensor_scalar(relx[:, :, :], xdt[:, :, :], 0.0, None, ALU.max).then_inc(relx_done, 1)
                    dve.wait_ge(relx_done, s + 1)
                    dve.scalar_tensor_tensor(floor[:, :, :], zexp[:, :, :], 0.5, relx[:, :, :], ALU.mult,
                                             ALU.add).then_inc(floor_done, 1)
                    dve.wait_ge(rest_done, s + 1)
                    dve.tensor_tensor(lp[:, :, :], rest[:, :, :], relx[:, :, :], ALU.add).then_inc(lpa, 1)

                def softplus_end(s, g):
                    dve.wait_ge(lnw_done, s + 1)
                    dve.wait_ge(lpa, s + 1)
                    dve.tensor_tensor(lp[:, :, :], lp[:, :, :], lnw[:, :, :], ALU.add).then_inc(lpb, 1)
                    dve.wait_ge(lpb, s + 1)
                    dve.wait_ge(floor_done, s + 1)
                    dve.tensor_tensor(dt[:, g, :, :], lp[:, :, :], floor[:, :, :], ALU.max).then_inc(dt_done, 1)
                    dve.wait_ge(dt_done, s + 1)
                    dve.tensor_tensor(u[:, g, :, :], dt[:, g, :, :], xc[:, g, :, :], ALU.mult).then_inc(u_done, 1)

                def mul(s, g, k):
                    p, c = k // C, k % C
                    n = UNITS * s + k
                    if k == 0:
                        dve.wait_ge(u_done, s + 1)
                    if c == 0:
                        dve.wait_ge(B_mm, PAIRS * s + p + 1)
                    if n >= 2:
                        dve.wait_ge(scan_done, n - 1)
                    dve.tensor_tensor(psD[:, n % 2, :].rearrange("p (i n) -> p i n", i=2),
                                      u[:, g, c:c + 1, :].to_broadcast([128, 2, GT]),
                                      psB[:, (PAIRS * s + p) % 2, :].rearrange("p (i n) -> p i n", i=2),
                                      ALU.mult).then_inc(mul_done, 1)

                def scan(s, k):
                    n = UNITS * s + k
                    dve.wait_ge(dA_done, n + 1)
                    dve.wait_ge(mul_done, n + 1)
                    if n >= RH:
                        dve.wait_ge(hC_done, n - RH + 1)
                    dve.tensor_tensor_scan(hs[:, n % RH, :], dA[:, n % RA, :], psD[:, n % 2, :], 0.0,
                                           ALU.mult, ALU.add).then_inc(scan_done, 1)

                def gate_a(s, l, g):
                    dve.wait_ge(y_mm, UNITS * (s + 1))
                    for c in range(C):
                        dve.scalar_tensor_tensor(ys[:, c, :], xc[:, g, c, :], sm_sb[:, l, c, SM_DP:SM_DP + 1], Y(c),
                                                 ALU.mult, ALU.add).then_inc(ys_done, 1)

                def gate_b(s, g):
                    dve.wait_ge(ys_done, C * (s + 1))
                    if s:
                        dve.wait_ge(out_mm, s)
                    dve.tensor_tensor(yg[:, :, :], ys[:, :, :], sz[:, g, :, :], ALU.mult).then_inc(yg_done, 1)

                def norm_stats(s):
                    dve.wait_ge(out_mm, s + 1)
                    for j in range(2):
                        dve.bn_stats(bst[:, j, :], psS[:, j * D:(j + 1) * D]).then_inc(bst_done, 1)
                    for j in range(2):
                        dve.wait_ge(bst_done, 2 * s + 1 + j)
                        dve.bn_aggr(mv[:, j, :], bst[:, j, :]).then_inc(mv_done, 1)

                def norm_apply(s, l, g):
                    dve.wait_ge(rstd_done, s + 1)
                    for j in range(2):
                        dve.tensor_scalar(nrm[:, j, :], psS[:, j * D:(j + 1) * D], mv[:, j, 0:1], rstd[:, j:j + 1],
                                          ALU.subtract, ALU.mult).then_inc(nrm_done, 1)
                    dve.wait_ge(nrm_done, 2 * (s + 1))
                    dve.tensor_tensor(nrmg[:, :, :], nrm[:, :, :],
                                      lngb_sb[:, l, 0:1, :].to_broadcast([128, 2, D]), ALU.mult).then_inc(nrmg_done, 1)
                    dve.wait_ge(nrmg_done, s + 1)
                    dve.wait_ge(resb_done, s + 1)
                    dve.tensor_tensor(xres[:, g, :, :], nrmg[:, :, :], resb[:, g, :, :], ALU.add).then_inc(x_done, 1)

                dve.memset(zeros[:, :], 0.0).then_inc(zeros_set, 1)
                dve.memset(dA[:, :, :], 0.0).then_inc(dA_zero, 1)
                dve.wait_ge(ld_const, 48)
                dve.wait_ge(ld_sm, 48)
                dve.tensor_scalar(acap_sb[:, :, :, :], alog_sb[:, :, :, :], A_LOG_MAX, None,
                                  ALU.min).then_inc(acap_done, 1)
                tok_out(0)
                conv_taps(0, 0, (0, 1))
                conv_taps(0, 0, (2,))
                split_bc(0, 0)
                split_bc2(0, 0)
                tok_out(1)
                softplus_round(0)
                softplus_floor(0)
                softplus_end(0, 0)
                for s in range(RUNS):
                    l, g = s // 2, s % 2
                    q = s + 1
                    ql, qg = q // 2, q % 2
                    mul(s, g, 0)
                    for k in range(UNITS):
                        if k + 1 < UNITS:
                            mul(s, g, k + 1)
                        scan(s, k)
                        if s > 0:
                            pl = (s - 1) // 2
                            if k == AT_DVE['gate']:
                                gate_a(s - 1, pl, 1 - g)
                                gate_b(s - 1, 1 - g)
                            if k == AT_DVE['stats']:
                                norm_stats(s - 1)
                            if k == AT_DVE['norm']:
                                norm_apply(s - 1, pl, 1 - g)
                        if q < RUNS:
                            if k == AT_DVE['conv_a']:
                                conv_taps(q, ql, (0, 1))
                            if k == AT_DVE['conv_b']:
                                conv_taps(q, ql, (2,))
                            if k == AT_DVE['split_a']:
                                split_bc(q, qg)
                            if k == AT_DVE['split_b']:
                                split_bc2(q, qg)
                            if k == AT_DVE['round']:
                                softplus_round(q)
                            if k == AT_DVE['floor']:
                                softplus_floor(q)
                            if k == AT_DVE['end']:
                                softplus_end(q, qg)
                s = RUNS - 1
                gate_a(s, LAYERS - 1, 1)
                gate_b(s, 1)
                norm_stats(s)
                norm_apply(s, LAYERS - 1, 1)

            @block.gpsimd
            def _(pool):
                pool.memset(mhalf[:, :], -0.5).then_inc(mhalf_set, 1)

                def res_bias(s, l, g):
                    pool.wait_ge(x_done, s + 1)
                    pool.tensor_tensor(resb[:, g, :, :], xres[:, g, :, :],
                                       lngb_sb[:, l, 1:2, :].to_broadcast([128, 2, D]), ALU.add).then_inc(resb_done, 1)

                def rstd_pow(s):
                    pool.wait_ge(mv_done, 2 * (s + 1))
                    if s:
                        pool.wait_ge(rstd_done, s)
                    pool.tensor_scalar(vpe[:, :], mv[:, :, 1], EPS, None, ALU.add).then_inc(vpe_done, 1)
                    pool.wait_ge(vpe_done, s + 1)
                    pool.tensor_tensor(rstd[:, :], vpe[:, :], mhalf[:, 0:2], ALU.pow).then_inc(rstd_done, 1)

                def log1p_rest(s):
                    pool.wait_ge(wm1_done, s + 1)
                    if s:
                        pool.wait_ge(lpa, s)
                    pool.tensor_tensor(rest[:, :, :], zexp[:, :, :], wm1[:, :, :], ALU.subtract).then_inc(rest_done, 1)

                def times_C(s, k):
                    p, c = k // C, k % C
                    n = UNITS * s + k
                    pool.wait_ge(scan_done, n + 1)
                    if c == 0:
                        pool.wait_ge(Cb_done, PAIRS * s + p + 1)
                    if n >= RC:
                        pool.wait_ge(y_mm, n - RC + 1)
                    pool.tensor_tensor(hC[:, n % RC, :], hs[:, n % RH, :], Cb[:, (PAIRS * s + p) % RCB, :],
                                       ALU.mult).then_inc(hC_done, 1)

                pool.wait_ge(mhalf_set, 1)
                pool.wait_ge(ld_sm, 48)
                log1p_rest(0)
                for s in range(RUNS):
                    l, g = s // 2, s % 2
                    for k in range(UNITS):
                        times_C(s, k)
                        if k == AT_POOL['res_bias']:
                            res_bias(s, l, g)
                        if s > 0 and k == AT_POOL['rstd']:
                            rstd_pow(s - 1)
                        if s + 1 < RUNS and k == AT_POOL['rest']:
                            log1p_rest(s + 1)
                rstd_pow(RUNS - 1)

        stack_ctx.close()
        hsum = sb("hsum", [128, TC, D])
        fst = sb("fst", [128, TC, 6])
        fmv = sb("fmv", [128, TC, 2])
        fvpe = sb("fvpe", [128, TC])
        frstd = sb("frstd", [128, TC])
        hh = sb("hh", [128, TC, D])
        hT = sb("hT", [DK, 2, NTOK])
        hT_hi, hT_lo = sb("hT_hi", [DK, 2, NTOK], fp32r), sb("hT_lo", [DK, 2, NTOK], fp32r)
        wi_hi, wi_lo = sb("wi_hi", [DK, 2, 2, F], fp32r), sb("wi_lo", [DK, 2, 2, F], fp32r)
        wo_hi, wo_lo = sb("wo_hi", [128, 2, FC, D], fp32r), sb("wo_lo", [128, 2, FC, D], fp32r)
        top = sb("top", [128, TC, 8])
        topi = sb("topi", [128, TC, 8], u32)
        topf = sb("topf", [128, TC, 8])
        gap = sb("gap", [128, TC])
        egap = sb("egap", [128, TC])
        den = sb("den", [128, TC])
        wtop = sb("wtop", [128, 2, TC])
        gw = sb("gw", [128, TC, E])
        gw2 = sb("gw2", [128, TC, E])
        gate = sb("gate", [128, TC, E])
        gateT = sb("gateT", [E, NTOK])
        RG = 4
        hg = sb("hg", [128, RG, NTOK])
        hg_hi, hg_lo = sb("hg_hi", [128, RG, NTOK], fp32r), sb("hg_lo", [128, RG, NTOK], fp32r)
        facc = sb("facc", [128, TC, D])
        fout = sb("fout", [128, TC, D])

        up = [psY[:, 0, :], psY[:, 1, :], psB[:, 0, :], psB[:, 1, :]]
        RU = len(up)
        down_banks = [(psD[:, 0, :], psD[:, 1, :]), (psC[:, :], psS[:, :])]

        def down(e, j):
            return down_banks[e % 2][j // 2][:, (j % 2) * D:(j % 2 + 1) * D]

        PARTS = ((0, 0), (0, 1), (1, 0))
        M = E * FC
        LAGD = 2

        with nc.Block() as block:

            @block.sync
            def _(sp):
                for e in range(2, E):
                    sp.wait_ge(wi_split, 2 * (e - 1))
                    sp.dma_start(wi_sb[:, e % 2, :, :], wi[e]).then_inc(ld_wi[e % 2], 16)
                    sp.wait_ge(wo_split, 2 * (e - 1))
                    sp.dma_start(wo_sb[:, e % 2, :, :], wo[e]).then_inc(ld_wo[e % 2], 16)
                sp.wait_ge(fin_done, TC)
                sp.dma_start(out.rearrange("(j p) d -> p j d", p=128), fout[:, :, :]).then_inc(out_done, 16)
                sp.wait_ge(out_done, 16)

            @block.tensor
            def _(pe):
                pe.wait_ge(hh_done, TC)
                for k in range(2):
                    for j in range(TC):
                        mm = pe.transpose(psB[0:DK, k, j * 128:(j + 1) * 128], hh[:, j, k * DK:(k + 1) * DK],
                                          ident[:, :])
                    mm.then_inc(hT_mm, 1)
                pe.wait_ge(hT_done, 2)
                pe.wait_ge(ld_ffn, 64)
                for j in range(TC):
                    for k in range(2):
                        mm = pe.matmul(psC[:, j * E:(j + 1) * E], hT[:, k, j * 128:(j + 1) * 128], wr_sb[:, k, :],
                                       start=(k == 0), stop=(k == 1))
                mm.then_inc(logit_mm, 1)

                def up_proj(m):
                    e, f = m // FC, m % FC
                    if f == 0:
                        pe.wait_ge(wi_split, 2 * (e + 1))
                    if m == 0:
                        pe.wait_ge(hT_split, 2)
                    if m >= RU:
                        pe.wait_ge(gelu_done, m - RU + 1)
                    i = 0
                    for k in range(2):
                        for a, b in PARTS:
                            mm = pe.matmul(up[m % RU], (wi_hi, wi_lo)[a][:, e % 2, k, f * 128:(f + 1) * 128],
                                           (hT_hi, hT_lo)[b][:, k, :], start=(i == 0), stop=(i == 5))
                            i += 1
                    mm.then_inc(up_mm, 1)

                def down_proj(m):
                    e, f = m // FC, m % FC
                    if f == 0:
                        pe.wait_ge(wo_split, 2 * (e + 1))
                        if e >= 1:
                            pe.wait_ge(facc_done, TC * e)
                        for bank in down_banks[e % 2]:
                            pe.matmul(bank, zeros[:, 0:128], zeros[:, :], start=True, stop=False,
                                      skip_group_check=True)
                    pe.wait_ge(hg_split, m + 1)
                    for j in range(TC):
                        for i, (a, b) in enumerate(PARTS):
                            mm = pe.matmul(down(e, j), (hg_hi, hg_lo)[a][:, m % RG, j * 128:(j + 1) * 128],
                                           (wo_hi, wo_lo)[b][:, e % 2, f, :], start=False,
                                           stop=(f == FC - 1 and i == 2), skip_group_check=True)
                    mm.then_inc(down_mm, 1)

                up_proj(0)
                up_proj(1)
                up_proj(2)
                pe.wait_ge(gate_done, 1)
                for j in range(TC):
                    mm = pe.transpose(psS[0:E, j * 128:(j + 1) * 128], gate[:, j, :], ident[:, :])
                mm.then_inc(gateT_mm, 1)
                pe.wait_ge(gateT_done, 1)
                for j in range(TC):
                    mm = pe.matmul(down(1, j), gateT[:, j * 128:(j + 1) * 128], bo_sb[:, :], start=True, stop=True)
                mm.then_inc(bo_mm, 1)
                for m in range(M + LAGD):
                    if 3 <= m < M:
                        up_proj(m)
                    if m >= LAGD:
                        down_proj(m - LAGD)

            @block.scalar
            def _(act):
                for k in range(2):
                    act.wait_ge(hT_mm, k + 1)
                    act.activation(hT[:, k, :], psB[0:DK, k, :], ACT.Copy).then_inc(hT_done, 1)
                act.wait_ge(gap_done, 1)
                act.activation(egap[:, :], gap[:, :], ACT.Exp).then_inc(egap_done, 1)

                def gelu(m):
                    e, f = m // FC, m % FC
                    act.wait_ge(up_mm, m + 1)
                    if m >= RG:
                        act.wait_ge(hg_split, m - RG + 1)
                    act.activation(hg[:, m % RG, :], up[m % RU], ACT.Gelu, bias=bi_sb[:, e, f:f + 1]).then_inc(gelu_done, 1)

                def hidden_hi(m):
                    act.wait_ge(gelu_done, m + 1)
                    if m >= RG:
                        act.wait_ge(down_mm, m - RG + 1)
                    act.activation(hg_hi[:, m % RG, :], hg[:, m % RG, :], ACT.Copy).then_inc(hghi_done, 1)

                gelu(0)
                gelu(1)
                hidden_hi(0)
                act.wait_ge(gateT_mm, 1)
                act.activation(gateT[:, :], psS[0:E, :], ACT.Copy).then_inc(gateT_done, 1)
                for m in range(2, M):
                    gelu(m)
                    hidden_hi(m - 1)
                hidden_hi(M - 1)

            @block.vector
            def _(dve):
                def split_weights(e):
                    sl = e % 2
                    for n, (w, hi, lo, ld, done) in enumerate(((wi_sb, wi_hi, wi_lo, ld_wi, wi_split),
                                                               (wo_sb, wo_hi, wo_lo, ld_wo, wo_split))):
                        dve.wait_ge(ld[sl], 16 * (e // 2 + 1))
                        if e >= 2:
                            dve.wait_ge(up_mm if n == 0 else down_mm, FC * (e - 1))
                        dve.tensor_copy(hi[:, sl, :, :], w[:, sl, :, :]).then_inc(done, 1)
                        dve.wait_ge(done, 2 * e + 1)
                        dve.tensor_tensor(lo[:, sl, :, :], w[:, sl, :, :], hi[:, sl, :, :].bitcast(fp32),
                                          ALU.subtract).then_inc(done, 1)

                def norm(i, src, dst, sums_done, done):
                    dve.wait_ge(sums_done[0], sums_done[1])
                    for j in range(TC):
                        dve.bn_stats(fst[:, j, :], src[:, j, :]).then_inc(fst_done, 1)
                    for j in range(TC):
                        dve.wait_ge(fst_done, TC * i + j + 1)
                        dve.bn_aggr(fmv[:, j, :], fst[:, j, :]).then_inc(fmv_done, 1)
                    dve.wait_ge(frstd_done, i + 1)
                    for j in range(TC):
                        dve.tensor_scalar(dst[:, j, :], src[:, j, :], fmv[:, j, 0:1], frstd[:, j:j + 1],
                                          ALU.subtract, ALU.mult).then_inc(done, 1)

                dve.wait_ge(x_done, RUNS + 2)
                dve.tensor_tensor(hsum[:, :, :], h0[:, :, :, :].rearrange("p g j d -> p (g j) d"),
                                  xres[:, :, :, :].rearrange("p g j d -> p (g j) d"), ALU.add).then_inc(hsum_done, 1)
                norm(0, hsum, hh, (hsum_done, 1), hh_done)
                split_weights(0)
                dve.wait_ge(hT_done, 2)
                dve.tensor_copy(hT_hi[:, :, :], hT[:, :, :]).then_inc(hT_split, 1)
                dve.wait_ge(hT_split, 1)
                dve.tensor_tensor(hT_lo[:, :, :], hT[:, :, :], hT_hi[:, :, :].bitcast(fp32),
                                  ALU.subtract).then_inc(hT_split, 1)

                dve.wait_ge(logit_mm, 1)
                for j in range(TC):
                    dve.max(top[:, j, :], psC[:, j * E:(j + 1) * E]).then_inc(top_done, 1)
                for j in range(TC):
                    dve.wait_ge(top_done, j + 1)
                    dve.max_index(topi[:, j, :], top[:, j, :], psC[:, j * E:(j + 1) * E]).then_inc(topi_done, 1)
                dve.tensor_tensor(gap[:, :], top[:, :, 1], top[:, :, 0], ALU.subtract).then_inc(gap_done, 1)
                dve.wait_ge(topi_done, TC)
                dve.tensor_copy(topf[:, :, :], topi[:, :, :]).then_inc(topf_done, 1)
                dve.wait_ge(egap_done, 1)
                dve.tensor_scalar(den[:, :], egap[:, :], 1.0, None, ALU.add).then_inc(den_done, 1)
                dve.wait_ge(den_done, 1)
                dve.reciprocal(wtop[:, 0, :], den[:, :]).then_inc(w1_done, 1)
                dve.wait_ge(w1_done, 1)
                dve.tensor_tensor(wtop[:, 1, :], egap[:, :], wtop[:, 0, :], ALU.mult).then_inc(w2_done, 1)
                dve.wait_ge(w2_done, 1)
                dve.wait_ge(topf_done, 1)
                dve.wait_ge(ld_ffn, 64)
                for i, dst in enumerate((gw, gw2)):
                    for j in range(TC):
                        dve.tensor_scalar(dst[:, j, :], iota_sb[:, :], topf[:, j, i:i + 1], wtop[:, i, j:j + 1],
                                          ALU.is_equal, ALU.mult).then_inc(gw_done, 1)
                dve.wait_ge(gw_done, 2 * TC)
                dve.tensor_tensor(gate[:, :, :], gw[:, :, :], gw2[:, :, :], ALU.add).then_inc(gate_done, 1)

                dve.wait_ge(bo_mm, 1)
                dve.wait_ge(hh_done, TC)
                for j in range(TC):
                    dve.tensor_tensor(facc[:, j, :], down(1, j), hh[:, j, :], ALU.add).then_inc(facc_done, 1)
                split_weights(1)
                for e in range(E):
                    if e + 2 < E:
                        pass
                    dve.wait_ge(down_mm, FC * (e + 1))
                    for j in range(TC):
                        dve.wait_ge(facc_done, TC * e + j + 1)
                        dve.scalar_tensor_tensor(facc[:, j, :], down(e, j), gate[:, j, e:e + 1], facc[:, j, :],
                                                 ALU.mult, ALU.add).then_inc(facc_done, 1)
                    if e + 2 < E:
                        split_weights(e + 2)
                norm(1, facc, fout, (facc_done, TC * (E + 1)), fin_done)

            @block.gpsimd
            def _(pool):
                def rstd_all(i):
                    pool.wait_ge(fmv_done, TC * (i + 1))
                    pool.tensor_scalar(fvpe[:, :], fmv[:, :, 1], EPS, None, ALU.add).then_inc(fvpe_done, 1)
                    pool.wait_ge(fvpe_done, i + 1)
                    pool.tensor_tensor(frstd[:, :], fvpe[:, :], mhalf[:, :], ALU.pow).then_inc(frstd_done, 1)

                rstd_all(0)
                for m in range(M):
                    pool.wait_ge(hghi_done, m + 1)
                    if m >= RG:
                        pool.wait_ge(down_mm, m - RG + 1)
                    pool.tensor_tensor(hg_lo[:, m % RG, :], hg[:, m % RG, :], hg_hi[:, m % RG, :].bitcast(fp32),
                                       ALU.subtract).then_inc(hg_split, 1)
                rstd_all(1)


_ORDER = ["patches", "tok_w", "tok_b", "in_w", "xp_w", "dt_w", "out_w", "lngb", "smalls", "a_log",
          "wr", "wi", "bi", "wo", "bo", "eye", "sel", "iota8"]


def kernel(**inputs):
    import numpy as _np
    import concourse.bacc as _bacc
    from concourse import mybir as _mybir
    from concourse.bass_utils import run_bass_kernel_spmd as _run

    def rows(m, k):
        m = m.reshape(m.shape[:-2] + (k, m.shape[-2] // k, m.shape[-1]))
        return _np.moveaxis(m, -3, -2)

    def on_all(m):
        return _np.repeat(m[None], 128, 0)

    i = {n: _np.asarray(v) for n, v in inputs.items()}
    at = {n[len("L0_attn_"):]: v for n, v in i.items() if n.startswith("L0_attn_")}
    ff = {n[len("L0_ffn_"):]: v for n, v in i.items() if n.startswith("L0_ffn_")}
    a = {}
    side = int(T ** 0.5)
    p = i["x"].shape[-1] // side
    pt = i["x"].reshape(B, 3, side, p, side, p).transpose(0, 2, 4, 3, 5, 1).reshape(NTOK, PATCH)
    a["patches"] = rows(pt.T, PC)
    a["tok_w"] = rows(i["L0_tok_W"].T, PC)
    a["tok_b"] = on_all(i["L0_tok_b"])
    a["in_w"] = rows(at["in_proj_w"].transpose(0, 2, 1), 2)
    xp = at["x_proj_w"]
    bc = xp[:, RANK:]
    pad = _np.zeros((LAYERS, 2 * NST - RANK, DI), xp.dtype)
    a["xp_w"] = rows(_np.concatenate([xp[:, :RANK], pad, bc, bc, bc], 1).transpose(0, 2, 1), C)
    a["dt_w"] = at["dt_proj_w"].transpose(0, 2, 1)
    a["out_w"] = rows(at["out_proj_w"].transpose(0, 2, 1), C)
    a["lngb"] = on_all(_np.stack([at["ln_g"], at["ln_b"]], 1))
    small = _np.concatenate([at["conv_w"], at["conv_b"][..., None], at["dt_proj_b"][..., None],
                             at["D_param"][..., None]], -1)
    a["smalls"] = small.reshape(LAYERS, C, 128, SM).transpose(2, 0, 1, 3)
    a["a_log"] = at["A_log"].reshape(LAYERS, C, 128, NST).transpose(2, 0, 1, 3)
    a["wr"] = rows(ff["Wr"].T, 2)
    a["wi"] = rows(ff["Wi"].transpose(0, 2, 1), 2)
    a["bi"] = ff["bi"].reshape(E, FC, 128).transpose(2, 0, 1)
    a["wo"] = rows(ff["Wo"].transpose(0, 2, 1), FC)
    a["bo"] = ff["bo"]
    a["iota8"] = on_all(_np.arange(E, dtype=_np.float32))
    a["eye"] = _np.eye(128, dtype=_np.float32)
    a["sel"] = _np.concatenate([_np.zeros((32, 32), _np.float32)] + 3 * [_np.eye(32, dtype=_np.float32)], 0)

    nc = _bacc.Bacc("TRN2", target_bir_lowering=False, num_devices=1)
    arrays, args = {}, []
    for n in _ORDER:
        arrays[f"in_{n}_dram"] = _np.ascontiguousarray(a[n])
        args.append(nc.dram_tensor(f"in_{n}_dram", a[n].shape, _mybir.dt.from_np(a[n].dtype),
                                   kind="ExternalInput").ap())
    args.append(nc.dram_tensor("out_0_dram", (NTOK, D), _mybir.dt.float32, kind="ExternalOutput").ap())
    tower_program(nc, *args)
    r = _run(nc, [arrays], core_ids=[0])
    return r.results[0]["out_0_dram"].reshape(B, T, D)
```

```python
import concourse.bass as bass
from concourse import mybir
from contextlib import ExitStack

LAYERS = 4
D = 192
DI = 384
NST = 16
RANK = 12
KCONV = 4
T = 16
B = 32
G = 2
GB = B // G
GT = GB * T
NTOK = B * T
C = DI // 128
DK = D // 2
PATCH = 768
PC = PATCH // 128
EPS = 1e-5
A_LOG_MAX = 80.0
PAIRS = NST // 2
UNITS = PAIRS * C
RUNS = LAYERS * G
LAG = 5
C_MM_LAG = -3
C_LAG = 1
AT_PE = dict(out_proj=2, transposes=6, pre_a=9, pre_b=10, pre_c=10, x_proj=13, dt_proj_a=14, dt_proj_b=15,
             skip=18)
AT_ACT = dict(normalize=7, raw_a=13, raw_b=15, raw_c=15, silus=15, x_proj_out=15, split_mid=20,
              split_low=23, dt_bias_a=19, dt_bias_b=19, exp=22, ln=23)
AT_DVE = dict(gate=0, stats=3, norm=7, conv_a=11, conv_b=11, round=22, rest=22, end=23)
AT_POOL = dict(res_bias=5, rstd=2, split_a=17, split_b=19)
LAST_PE = dict(x_back_0=8, x_back_1=11, h_transposes=20)
LAST_ACT = dict(h_copy=21)
LAST_DVE = dict(gate=0, stats=5, centre=8, sum_0=10, base_1=11, h_stats=14, h_norm=17, h_parts=23)
LAST_POOL = dict(rstd=4, h_scale=14)
E = 8
F = 768
FC = F // 128
TC = NTOK // 128
SM_CONVW, SM_CONVB, SM_DTB, SM_DP = 0, 4, 5, 6
SM = 7


def tower_program(nc, patches, tok_w, tok_b, in_w, xp_w, dt_w, out_w, lngb, smalls, a_log,
                  wr, wi, bi, wo, bo, eye, sel, iota8, last_g, out):
    fp32 = mybir.dt.float32
    bf16 = mybir.dt.bfloat16
    u32 = mybir.dt.uint32
    fp32r = mybir.dt.float32r
    ALU = mybir.AluOpType
    ACT = mybir.ActivationFunctionType

    RA, RB, RH, RC, RCB = 8, 3, 6, 6, 4

    ctx = ExitStack()
    with ctx:
        stack_ctx = ExitStack()

        def sb(name, shape, dt=fp32):
            return ctx.enter_context(nc.sbuf_tensor(name, shape, dt))

        def sbs(name, shape, dt=fp32):
            return stack_ctx.enter_context(nc.sbuf_tensor(name, shape, dt))

        def pb(name, shape, dt=fp32):
            return ctx.enter_context(nc.psum_tensor(name, shape, dt))

        def sem(name):
            return ctx.enter_context(nc.semaphore(name))

        ident = sb("ident", [128, 128])
        zeros = sb("zeros", [128, 512], bf16)
        mhalf = sb("mhalf", [128, TC])
        h0 = sb("h0", [128, G, 2, D])
        xT = sb("xT", [DK, G, 2, GT])
        iota_sb = sb("iota_sb", [128, E])
        wr_sb = sb("wr_sb", [128, 2, E])
        bo_sb = sb("bo_sb", [2 * E, D])
        bi_sb = sb("bi_sb", [128, E, FC])
        wi_sb = sb("wi_sb", [128, 2, 2, F])
        wo_sb = sb("wo_sb", [128, 2, FC, D])

        pat_sb = sb("pat_sb", [128, PC, NTOK])
        tokw_sb = sb("tokw_sb", [128, PC, D])
        xh = sb("xh", [128, TC, D])
        lng_row = sb("lng_row", [128, D])
        fst = sb("fst", [128, TC, 6])
        fmv = sb("fmv", [128, TC, 2])
        fvpe = sb("fvpe", [128, TC])
        frstd = sb("frstd", [128, TC])
        hT_hi, hT_lo = sb("hT_hi", [128, 2, NTOK], fp32r), sb("hT_lo", [128, 2, NTOK], fp32r)
        hsum = tokw_sb[:, 0:TC, :]
        hT = pat_sb[:, 0:2, :]
        hh = pat_sb[:, 2:4, :].rearrange("p k (j d) -> p (k j) d", j=2)
        xTb = pat_sb[0:DK, 4:6, :].rearrange("p g (k n) -> p g k n", k=2)

        selc = sbs("selc", [128, 2 * NST])
        sel_sb = sbs("sel_sb", [128, 2 * NST, 128], bf16)
        tokb_sb = sbs("tokb_sb", [128, D])
        sm_sb = sbs("sm_sb", [128, LAYERS, C, SM])
        alog_sb = sbs("alog_sb", [128, LAYERS, C, NST])
        acap_sb = sbs("acap_sb", [128, LAYERS, C, NST])
        ea_sb = sbs("ea_sb", [128, LAYERS, C, NST])
        na_sb = sbs("na_sb", [128, LAYERS, C, NST])
        dpd = sbs("dpd", [128, LAYERS, C, 128])
        lngb_sb = sbs("lngb_sb", [DK, LAYERS, 2, 2])
        inw_sb = sbs("inw_sb", [DK, 2, 2 * DI])
        xpw_sb = sbs("xpw_sb", [128, C, 128])
        dtw_sb = sbs("dtw_sb", [RANK, DI])
        outw_sb = sbs("outw_sb", [128, C, D])
        raw = sbs("raw", [128, 2 * C, GT])
        acc = sbs("acc", [128, C, GT])
        xc = sbs("xc", [128, G, C, GT])
        sz = sbs("sz", [128, G, C, GT])
        dtlow = sbs("dtlow", [RANK, GT])
        BC = sbs("BC", [128, G, GT], bf16)
        BCf = sbs("BCf", [128, GT])
        rem = sbs("rem", [128, GT])
        rem2 = sbs("rem2", [128, GT])
        xdt = sbs("xdt", [128, C, GT])
        zexp = sbs("zexp", [128, C, GT])
        lnw = sbs("lnw", [128, C, GT])
        wm1 = sbs("wm1", [128, C, GT])
        lp = sbs("lp", [128, C, GT])
        rest = sbs("rest", [128, C, GT])
        dt = sbs("dt", [128, G, C, GT])
        u = sbs("u", [128, G, C, GT])
        dA = sbs("dA", [128, RA, 2 * GT])
        uB = sbs("uB", [128, RB, 2 * GT])
        hs = sbs("hs", [128, RH, 2 * GT])
        hC = sbs("hC", [128, RC, 2 * GT])
        Cb = sbs("Cb", [128, RCB, 2 * GT])
        yg = sbs("yg", [128, C, GT])
        bst = sbs("bst", [128, 2, 6])
        mv = sbs("mv", [128, 2, 2])
        vpe = sbs("vpe", [128, 2])
        rstd = sbs("rstd", [128, 2])
        nrm = sbs("nrm", [128, 2, D])
        nmean = sbs("nmean", [128, 2])
        nmr = sbs("nmr", [128, 2])

        psY = pb("psY", [128, 2, 512])
        psB = pb("psB", [128, 2, 512])
        psC = pb("psC", [128, 512])
        psS, psT, psU = pb("psS", [128, 512]), pb("psT", [128, 512]), pb("psU", [128, 512])

        def Y(c):
            return psY[:, c // 2, (c % 2) * GT:(c % 2 + 1) * GT]

        in_bank = (psU, psS, psT)
        tok_bank, xT_bank = (psS, psY[:, 0, :]), (psT, psY[:, 1, :])
        x_bank = (psT, psU)

        def bt(ap):
            return ap.rearrange("p (b t) -> p b t", t=T)

        ld_const, ld_tok, ld_sm = sem("ld_const"), [sem("ld_tok0"), sem("ld_tok1")], sem("ld_sm")
        ld_pre, ld_post = sem("ld_pre"), sem("ld_post")
        zeros_set, dA_zero, mhalf_set, acap_done = sem("zeros_set"), sem("dA_zero"), sem("mhalf_set"), sem("acap_done")
        sel_done = sem("sel_done")
        ea_done, na_done = sem("ea_done"), sem("na_done")
        tok_mm, h0_done = sem("tok_mm"), sem("h0_done")
        xT_mm, xT_done = sem("xT_mm"), sem("xT_done")
        in_mm = sem("in_mm")
        conv0, conv1, conv2, conv3 = sem("conv0"), sem("conv1"), sem("conv2"), sem("conv3")
        z_done, xc_done = sem("z_done"), sem("xc_done")
        xp_mm, dtlow_done, bc_hi_done = sem("xp_mm"), sem("dtlow_done"), sem("bc_hi_done")
        rem_done, bc_mid_done, rem2_done, bc_lo_done = (sem("rem_done"), sem("bc_mid_done"), sem("rem2_done"),
                                                        sem("bc_lo_done"))
        dt_mm, abs_done, xdt_done, raw_done = sem("dt_mm"), sem("abs_done"), sem("xdt_done"), sem("raw_done")
        zexp_done, lnw_done, wm1_done = sem("zexp_done"), sem("lnw_done"), sem("wm1_done")
        lp_sum_done, lp_done, rest_done = sem("lp_sum_done"), sem("lp_done"), sem("rest_done")
        bcf_done, xTb_done = sem("bcf_done"), sem("xTb_done")
        nmean_done, nmr_done, nT_mm = sem("nmean_done"), sem("nmr_done"), sem("nT_mm")
        dt_done, u_done = sem("dt_done"), sem("u_done")
        B_mm, C_mm, Cb_done = sem("B_mm"), sem("C_mm"), sem("Cb_done")
        dA_done, mul_done, scan_done, hC_done, y_mm = (sem("dA_done"), sem("mul_done"), sem("scan_done"),
                                                       sem("hC_done"), sem("y_mm"))
        dpd_done, yg_done, out_mm, bst_done, mv_done = (sem("dpd_done"), sem("yg_done"), sem("out_mm"),
                                                       sem("bst_done"), sem("mv_done"))
        vpe_done, rstd_done, nrm_done = sem("vpe_done"), sem("rstd_done"), sem("nrm_done")
        out_done = sem("out_done")
        ld_ffn, ld_wi, ld_wo = sem("ld_ffn"), [sem("ld_wi0"), sem("ld_wi1")], [sem("ld_wo0"), sem("ld_wo1")]
        hsum_done, fst_done, fmv_done = sem("hsum_done"), sem("fst_done"), sem("fmv_done")
        fvpe_done, frstd_done, hh_done = sem("fvpe_done"), sem("frstd_done"), sem("hh_done")
        hT_mm, hT_done, logit_mm = sem("hT_mm"), sem("hT_done"), sem("logit_mm")
        top_done, topi_done, gap_done, egap_done = (sem("top_done"), sem("topi_done"), sem("gap_done"),
                                                    sem("egap_done"))
        topf_done, den_done, w1_done, w2_done = sem("topf_done"), sem("den_done"), sem("w1_done"), sem("w2_done")
        gw_done, gate_done, gateT_mm, gateT_done = (sem("gw_done"), sem("gate_done"), sem("gateT_mm"),
                                                    sem("gateT_done"))
        facc_done, facc2_done, pick_done = sem("facc_done"), sem("facc2_done"), sem("pick_done")
        up_mm, up_read, gated, down_mm, y_all = sem("up_mm"), sem("up_read"), sem("gated"), sem("down_mm"), sem("y_all")
        gate_split = sem("gate_split")
        fin_done, xback_mm, xh_done, centred = sem("fin_done"), sem("xback_mm"), sem("xh_done"), sem("centred")
        wi_split, wo_split, hT_split, hghi_done, hg_split = (sem("wi_split"), sem("wo_split"), sem("hT_split"),
                                                             sem("hghi_done"), sem("hg_split"))
        LDPRE, LDPOST = 3 * 16, 1 * 16
        LDFFN = 5 * 16

        def h_stats(dve, g):
            for j in range(2 * g, 2 * g + 2):
                dve.wait_ge(hsum_done, j + 1)
                dve.bn_stats(fst[:, j, :], hsum[:, j, :]).then_inc(fst_done, 1)
            for j in range(2 * g, 2 * g + 2):
                dve.wait_ge(fst_done, j + 1)
                dve.bn_aggr(fmv[:, j, :], fst[:, j, :]).then_inc(fmv_done, 1)

        def h_scale(pool, g):
            js = slice(2 * g, 2 * g + 2)
            pool.wait_ge(fmv_done, 2 * (g + 1))
            pool.tensor_scalar(fvpe[:, js], fmv[:, js, 1], EPS, None, ALU.add).then_inc(fvpe_done, 1)
            pool.wait_ge(fvpe_done, g + 1)
            pool.tensor_tensor(frstd[:, js], fvpe[:, js], mhalf[:, js], ALU.pow).then_inc(frstd_done, 1)

        def h_norm(dve, g):
            dve.wait_ge(frstd_done, g + 1)
            for j in range(2 * g, 2 * g + 2):
                dve.tensor_scalar(hh[:, j, 0:D], hsum[:, j, :], fmv[:, j, 0:1], frstd[:, j:j + 1],
                                  ALU.subtract, ALU.mult).then_inc(hh_done, 1)
            dve.wait_ge(hh_done, 3 * g + 2)
            dve.tensor_copy(hh[:, 2 * g:2 * g + 2, D:256], hh[:, 2 * g:2 * g + 2, 128:D]).then_inc(hh_done, 1)

        def h_transposes(pe, g):
            for part in range(2):
                pe.wait_ge(hh_done, 3 * g + 2 + part)
                for j in range(2):
                    mm = pe.transpose(psT[:, part * GT + j * 128:part * GT + (j + 1) * 128],
                                      hh[:, 2 * g + j, part * 128:(part + 1) * 128], ident[:, :])
            mm.then_inc(hT_mm, 1)

        def h_copy(act, g):
            act.wait_ge(hT_mm, g + 1)
            act.activation(hT[:, :, g * GT:(g + 1) * GT], psT[:, :].rearrange("p (k n) -> p k n", k=2),
                           ACT.Copy).then_inc(hT_done, 1)

        def h_parts(dve, g):
            cols = slice(g * GT, (g + 1) * GT)
            dve.wait_ge(hT_done, g + 1)
            dve.tensor_copy(hT_hi[:, :, cols], hT[:, :, cols]).then_inc(hT_split, 1)
            dve.wait_ge(hT_split, 2 * g + 1)
            dve.tensor_tensor(hT_lo[:, :, cols], hT[:, :, cols], hT_hi[:, :, cols].bitcast(fp32),
                              ALU.subtract).then_inc(hT_split, 1)

        with nc.Block() as block:

            @block.sync
            def _(sp):
                sp.dma_start(tokw_sb[:, :, :], tok_w).then_inc(ld_tok[0], 16)
                for j in range(PC):
                    sp.dma_start(pat_sb[:, j, 0:GT], patches[:, j, 0:GT]).then_inc(ld_tok[0], 16)
                sp.dma_start(tokb_sb[:, :], tok_b).then_inc(ld_const, 16)
                sp.dma_start(ident[:, :], eye).then_inc(ld_const, 16)
                sp.dma_start(selc[:, :], sel).then_inc(ld_const, 16)
                sp.dma_start(sm_sb[:, :, :, :], smalls).then_inc(ld_sm, 16)
                sp.dma_start(alog_sb[:, :, :, :], a_log).then_inc(ld_sm, 16)
                sp.dma_start(lngb_sb[:, :, :, :], lngb).then_inc(ld_sm, 16)

                def load_pre(l):
                    if l:
                        sp.wait_ge(dt_mm, 2 * 2 * l)
                    sp.dma_start(inw_sb[:, :, :], in_w[l]).then_inc(ld_pre, 16)
                    sp.dma_start(xpw_sb[:, :, :], xp_w[l]).then_inc(ld_pre, 16)
                    sp.dma_start(dtw_sb[:, :], dt_w[l]).then_inc(ld_pre, 16)

                def load_post(l):
                    if l:
                        sp.wait_ge(out_mm, 2 * l)
                    sp.dma_start(outw_sb[:, :, :], out_w[l]).then_inc(ld_post, 16)

                load_pre(0)
                for j in range(PC):
                    sp.dma_start(pat_sb[:, j, GT:], patches[:, j, GT:]).then_inc(ld_tok[1], 16)
                load_post(0)
                sp.dma_start(iota_sb[:, :], iota8).then_inc(ld_ffn, 16)
                sp.dma_start(wr_sb[:, :, :], wr).then_inc(ld_ffn, 16)
                sp.dma_start(bo_sb[:, :], bo).then_inc(ld_ffn, 16)
                sp.dma_start(bi_sb[:, :, :], bi).then_inc(ld_ffn, 16)
                sp.dma_start(lng_row[:, :], last_g).then_inc(ld_ffn, 16)
                for e in range(2):
                    sp.dma_start(wi_sb[:, e, :, :], wi[e]).then_inc(ld_wi[e], 16)
                    sp.dma_start(wo_sb[:, e, :, :], wo[e]).then_inc(ld_wo[e], 16)
                for l in range(1, LAYERS):
                    load_pre(l)
                    load_post(l)

            @block.tensor
            def _(pe):
                def tok(g):
                    pe.wait_ge(ld_tok[g], 16 * (1 + PC) if g == 0 else 16 * PC)
                    for j in range(2):
                        lo = g * GT + j * 128
                        for k in range(PC):
                            mm = pe.matmul(tok_bank[g][:, j * D:(j + 1) * D], pat_sb[:, k, lo:lo + 128],
                                           tokw_sb[:, k, :], start=(k == 0), stop=(k == PC - 1))
                    mm.then_inc(tok_mm, 1)

                def tok_transposes(g):
                    pe.wait_ge(h0_done, g + 1)
                    for k in range(2):
                        for j in range(2):
                            mm = pe.transpose(xT_bank[g][0:DK, k * GT + j * 128:k * GT + (j + 1) * 128],
                                              h0[:, g, j, k * DK:(k + 1) * DK], ident[:, :])
                    mm.then_inc(xT_mm, 1)

                def norm_transposes(s):
                    pe.wait_ge(nrm_done, 2 * (s + 1))
                    for k in range(2):
                        for j in range(2):
                            mm = pe.transpose(psT[0:DK, k * GT + j * 128:k * GT + (j + 1) * 128],
                                              nrm[:, j, k * DK:(k + 1) * DK], ident[:, :])
                    mm.then_inc(nT_mm, 1)

                def in_proj(s, g, i):
                    e, bank = 2 * i, in_bank[i]
                    for h in range(2):
                        for k in range(2):
                            mm = pe.matmul(bank[:, h * GT:(h + 1) * GT],
                                           inw_sb[:, k, (e + h) * 128:(e + h + 1) * 128], xT[:, g, k, :],
                                           start=(k == 0), stop=(k == 1))
                    mm.then_inc(in_mm, 1)

                def pre_a(s, g, l):
                    pe.wait_ge(ld_pre, LDPRE * (l + 1))
                    pe.wait_ge(xT_done, s + 1)
                    in_proj(s, g, 0)

                def pre_b(s, g):
                    in_proj(s, g, 1)

                def pre_c(s, g):
                    in_proj(s, g, 2)

                def x_proj(s, g):
                    pe.wait_ge(xc_done, s + 1)
                    pe.wait_ge(raw_done, C * (s + 1))
                    for c in range(C):
                        mm = pe.matmul(psU[:, 0:GT], xpw_sb[:, c, :], xc[:, g, c, :], start=(c == 0), stop=(c == C - 1))
                    mm.then_inc(xp_mm, 1)

                def dt_proj_a(s):
                    pe.wait_ge(dtlow_done, s + 1)
                    for c in range(2):
                        mm = pe.matmul(psS[:, c * GT:(c + 1) * GT], dtw_sb[:, c * 128:(c + 1) * 128], dtlow[:, :],
                                       start=True, stop=True)
                    mm.then_inc(dt_mm, 1)

                def dt_proj_b(s):
                    pe.matmul(psT[:, 0:GT], dtw_sb[:, 256:384], dtlow[:, :], start=True, stop=True).then_inc(dt_mm, 1)

                def out_proj(s, l):
                    pe.wait_ge(yg_done, 2 * (s + 1))
                    pe.wait_ge(ld_post, LDPOST * (l + 1))
                    pe.wait_ge(xdt_done, C * min(s + 2, RUNS))
                    for j in range(2):
                        for c in range(C):
                            mm = pe.matmul(psS[:, j * D:(j + 1) * D], yg[:, c, j * 128:(j + 1) * 128], outw_sb[:, c, :],
                                           start=(c == 0), stop=(c == C - 1))
                    mm.then_inc(out_mm, 1)

                def broadcast_B(s, g, p):
                    n = PAIRS * s + p
                    if n == 0:
                        pe.wait_ge(sel_done, 1)
                    if p == 0:
                        pe.wait_ge(bc_lo_done, s + 1)
                    if n >= 2:
                        pe.wait_ge(mul_done, C * (n - 1))
                    for i in range(2):
                        mm = pe.matmul(psB[:, n % 2, i * GT:(i + 1) * GT], sel_sb[:, 2 * p + i, :], BC[:, g, :],
                                       start=True, stop=True)
                    mm.then_inc(B_mm, 1)

                def broadcast_C(s, g, p):
                    n = PAIRS * s + p
                    if n >= 1:
                        pe.wait_ge(Cb_done, n)
                    for i in range(2):
                        mm = pe.matmul(psC[:, i * GT:(i + 1) * GT], sel_sb[:, NST + 2 * p + i, :], BC[:, g, :],
                                       start=True, stop=True)
                    mm.then_inc(C_mm, 1)

                def y_clear(s):
                    if s:
                        pe.wait_ge(yg_done, 2 * s)
                    else:
                        pe.wait_ge(h0_done, 2)
                        pe.wait_ge(xT_done, 2)
                    for i in range(2):
                        pe.matmul(psY[:, i, :], zeros[:, 0:128], zeros[:, :], start=True, stop=False,
                                  skip_group_check=True)

                def y_sum(s, k):
                    n = UNITS * s + k
                    pe.wait_ge(hC_done, n + 1)
                    for i in range(2):
                        mm = pe.matmul(Y(k % C), ident[:, :], hC[:, n % RC, i * GT:(i + 1) * GT],
                                       start=False, stop=(k >= UNITS - C and i == 1), skip_group_check=True)
                    mm.then_inc(y_mm, 1)

                def y_skip(s, g, l):
                    if s == 0:
                        pe.wait_ge(dpd_done, LAYERS * C)
                    for c in range(C):
                        pe.matmul(Y(c), dpd[:, l, c, :], xc[:, g, c, :], start=False, stop=False,
                                  skip_group_check=True)

                def x_back(g):
                    pe.wait_ge(xTb_done, RUNS - 1 + g)
                    for j in range(2):
                        for k in range(2):
                            mm = pe.transpose(x_bank[g][:, j * D + k * DK:j * D + (k + 1) * DK],
                                              xTb[:, g, k, j * 128:(j + 1) * 128], ident[0:DK, 0:DK])
                    mm.then_inc(xback_mm, 1)

                pe.wait_ge(zeros_set, 1)
                for i in range(14):
                    pe.matmul(psB[:, 0, :], zeros[:, 0:128], zeros[:, :], start=True, stop=True)
                pe.wait_ge(ld_const, 48)
                tok(0)
                tok_transposes(0)
                pre_a(0, 0, 0)
                pre_b(0, 0)
                pre_c(0, 0)
                tok(1)
                x_proj(0, 0)
                dt_proj_a(0)
                dt_proj_b(0)
                tok_transposes(1)
                for s in range(RUNS):
                    l, g = s // 2, s % 2
                    for k in range(UNITS + LAG):
                        for p in range(PAIRS):
                            if k == max(0, C * (p - 1)):
                                broadcast_B(s, g, p)
                            if k == max(0, C * p + C_MM_LAG):
                                broadcast_C(s, g, p)
                        if k == LAG:
                            y_clear(s)
                        if k >= LAG:
                            y_sum(s, k - LAG)
                        if k == AT_PE['skip']:
                            y_skip(s, g, l)
                        if s > 0:
                            if k == AT_PE['out_proj']:
                                out_proj(s - 1, (s - 1) // 2)
                            if k == AT_PE['transposes'] and s < RUNS - 1:
                                norm_transposes(s - 1)
                        if s == RUNS - 1:
                            if k == LAST_PE['x_back_0']:
                                x_back(0)
                            if k == LAST_PE['x_back_1']:
                                x_back(1)
                            if k == LAST_PE['h_transposes']:
                                h_transposes(pe, 0)
                        if s + 1 < RUNS:
                            q = s + 1
                            if k == AT_PE['pre_a']:
                                pre_a(q, 1 - g, q // 2)
                            if k == AT_PE['pre_b']:
                                pre_b(q, 1 - g)
                            if k == AT_PE['pre_c']:
                                pre_c(q, 1 - g)
                            if k == AT_PE['x_proj']:
                                x_proj(q, 1 - g)
                            if k == AT_PE['dt_proj_a']:
                                dt_proj_a(q)
                            if k == AT_PE['dt_proj_b']:
                                dt_proj_b(q)
                out_proj(RUNS - 1, LAYERS - 1)

            @block.scalar
            def _(act):
                def xT_copy(g):
                    act.wait_ge(xT_mm, g + 1)
                    act.activation(xT[:, g, :, :], xT_bank[g][0:DK, :].rearrange("p (k n) -> p k n", k=2),
                                   ACT.Copy).then_inc(xT_done, 1)

                def normalize(s):
                    act.wait_ge(rstd_done, s + 1)
                    act.wait_ge(nmr_done, s + 1)
                    if s:
                        act.wait_ge(nT_mm, s)
                    for j in range(2):
                        act.activation(nrm[:, j, :], psS[:, j * D:(j + 1) * D], ACT.Identity,
                                       scale=rstd[:, j:j + 1], bias=nmr[:, j:j + 1]).then_inc(nrm_done, 1)

                def raw_copy(s, i):
                    act.wait_ge(in_mm, C * s + i + 1)
                    if s and i == 0:
                        act.wait_ge(conv3, C * s)
                        act.wait_ge(z_done, s)
                    act.activation(raw[:, 2 * i:2 * i + 2, :], in_bank[i].rearrange("p (i n) -> p i n", i=2),
                                   ACT.Copy).then_inc(raw_done, 1)

                def conv_last_tap(s, l, c):
                    act.wait_ge(raw_done, C * s + c // 2 + 1)
                    if c == 0 and s > 0:
                        act.wait_ge(xc_done, s)
                    act.activation(acc[:, c, :], raw[:, c, :], ACT.Identity,
                                   scale=sm_sb[:, l, c, SM_CONVW + 3:SM_CONVW + 4],
                                   bias=sm_sb[:, l, c, SM_CONVB:SM_CONVB + 1]).then_inc(conv0, 1)

                def silus(s, g):
                    act.wait_ge(conv3, C * (s + 1))
                    act.activation(xc[:, g, :, :], acc[:, :, :], ACT.Silu).then_inc(xc_done, 1)
                    act.wait_ge(raw_done, C * (s + 1))
                    act.activation(sz[:, g, :, :], raw[:, C:2 * C, :], ACT.Silu).then_inc(z_done, 1)
                    exp_ln_tables()

                def x_proj_out(s, g):
                    act.wait_ge(xp_mm, s + 1)
                    if s:
                        act.wait_ge(dt_mm, 2 * s)
                        act.wait_ge(rem_done, s)
                    act.activation(dtlow[:, :], psU[0:RANK, 0:GT], ACT.Copy).then_inc(dtlow_done, 1)
                    act.activation(BCf[:, :], psU[:, 0:GT], ACT.Copy).then_inc(bcf_done, 1)
                    act.wait_ge(bcf_done, s + 1)
                    act.activation(BC[:, g, :], BCf[:, :], ACT.Copy).then_inc(bc_hi_done, 1)

                def split_mid(s, g):
                    act.wait_ge(rem_done, s + 1)
                    act.activation(BC[64:128, g, :], rem[64:128, :], ACT.Copy).then_inc(bc_mid_done, 1)

                def split_low(s, g):
                    act.wait_ge(rem2_done, s + 1)
                    act.activation(BC[96:128, g, :], rem2[96:128, :], ACT.Copy).then_inc(bc_lo_done, 1)

                def dt_bias(s, l, c):
                    act.wait_ge(dt_mm, 2 * s + c // 2 + 1)
                    if c == 0 and s > 0:
                        act.wait_ge(dt_done, C * s)
                    act.activation(xdt[:, c, :], (psS, psS[:, GT:], psT)[c][:, 0:GT], ACT.Identity,
                                   bias=sm_sb[:, l, c, SM_DTB:SM_DTB + 1]).then_inc(xdt_done, 1)

                def exp_ln_tables():
                    act.preload_act_table_set("natural_log_exp_and_others")

                def softplus_exp(s):
                    act.wait_ge(xdt_done, C * (s + 1))
                    if s:
                        act.wait_ge(lp_done, s)
                    act.activation(zexp[:, :, :], xdt[:, :, :], ACT.Abs).then_inc(abs_done, 1)
                    act.wait_ge(abs_done, s + 1)
                    act.activation(zexp[:, :, :], zexp[:, :, :], ACT.Exp, scale=-1.0).then_inc(zexp_done, 1)

                def softplus_ln(s):
                    act.wait_ge(zexp_done, s + 1)
                    if s:
                        act.wait_ge(lp_sum_done, s)
                    act.activation(lnw[:, :, :], zexp[:, :, :], ACT.Ln, bias=1.0).then_inc(lnw_done, 1)

                def decay(s, l, g, k):
                    p, c = k // C, k % C
                    n = UNITS * s + k
                    if p == 0:
                        act.wait_ge(dt_done, C * s + c + 1)
                    if n >= RA:
                        act.wait_ge(scan_done, n - RA + 1)
                    for i in range(2):
                        st = 2 * p + i
                        a = act.activation(bt(dA[:, n % RA, i * GT:(i + 1) * GT])[:, :, 1:T],
                                           bt(dt[:, g, c, :])[:, :, 1:T], ACT.Exp,
                                           scale=na_sb[:, l, c, st:st + 1])
                    a.then_inc(dA_done, 1)

                def C_copy(s, p):
                    n = PAIRS * s + p
                    act.wait_ge(C_mm, n + 1)
                    if n >= RCB:
                        act.wait_ge(hC_done, C * (n - RCB + 1))
                    act.activation(Cb[:, n % RCB, :], psC[:, :], ACT.Copy).then_inc(Cb_done, 1)

                act.wait_ge(ld_const, 48)
                act.activation(sel_sb[:, :, :], selc[:, :].rearrange("p (n o) -> p n o", o=1)
                               .to_broadcast([128, 2 * NST, 128]), ACT.Copy).then_inc(sel_done, 1)
                act.wait_ge(ld_sm, 48)
                act.wait_ge(acap_done, 1)
                act.activation(ea_sb[:, :, :, :], acap_sb[:, :, :, :], ACT.Exp).then_inc(ea_done, 1)
                act.wait_ge(ea_done, 1)
                act.activation(na_sb[:, :, :, :], ea_sb[:, :, :, :], ACT.Copy, scale=-1.0).then_inc(na_done, 1)
                xT_copy(0)
                raw_copy(0, 0)
                for c in range(2):
                    conv_last_tap(0, 0, c)
                raw_copy(0, 1)
                conv_last_tap(0, 0, 2)
                raw_copy(0, 2)
                silus(0, 0)
                x_proj_out(0, 0)
                for c in range(C):
                    dt_bias(0, 0, c)
                split_mid(0, 0)
                softplus_exp(0)
                split_low(0, 0)
                softplus_ln(0)
                xT_copy(1)
                act.wait_ge(na_done, 1)
                act.wait_ge(dA_zero, 1)
                for s in range(RUNS):
                    l, g = s // 2, s % 2
                    q = s + 1
                    for k in range(UNITS):
                        for p in range(PAIRS):
                            if k == max(0, C * p + C_LAG):
                                C_copy(s, p)
                        decay(s, l, g, k)
                        if 0 < s < RUNS - 1 and k == AT_ACT['normalize']:
                            normalize(s - 1)
                        if s == RUNS - 1 and k == LAST_ACT['h_copy']:
                            h_copy(act, 0)
                        if q < RUNS:
                            ql, qg = q // 2, q % 2
                            if k == AT_ACT['split_mid']:
                                split_mid(q, qg)
                            if k == AT_ACT['split_low']:
                                split_low(q, qg)
                            if k == AT_ACT['raw_a']:
                                raw_copy(q, 0)
                                conv_last_tap(q, ql, 0)
                                conv_last_tap(q, ql, 1)
                            if k == AT_ACT['raw_b']:
                                raw_copy(q, 1)
                                conv_last_tap(q, ql, 2)
                            if k == AT_ACT['raw_c']:
                                raw_copy(q, 2)
                            if k == AT_ACT['silus']:
                                silus(q, qg)
                            if k == AT_ACT['x_proj_out']:
                                x_proj_out(q, qg)
                            if k == AT_ACT['dt_bias_a']:
                                dt_bias(q, ql, 0)
                                dt_bias(q, ql, 1)
                            if k == AT_ACT['dt_bias_b']:
                                dt_bias(q, ql, 2)
                            if k == AT_ACT['exp']:
                                softplus_exp(q)
                            if k == AT_ACT['ln']:
                                softplus_ln(q)
                    for p in range(PAIRS):
                        if C * p + C_LAG >= UNITS:
                            C_copy(s, p)

            @block.vector
            def _(dve):
                def tok_out(g):
                    dve.wait_ge(tok_mm, g + 1)
                    for j in range(2):
                        t = dve.tensor_tensor(h0[:, g, j, :], tok_bank[g][:, j * D:(j + 1) * D], tokb_sb[:, :], ALU.add)
                    t.then_inc(h0_done, 1)

                def conv_taps(s, l, cs):
                    sems = [conv1, conv2, conv3]
                    for k in range(1, KCONV):
                        for c in cs:
                            dve.wait_ge([conv0, conv1, conv2][k - 1], C * s + c + 1)
                            av = bt(acc[:, c, :])[:, :, k:T]
                            dve.scalar_tensor_tensor(av, bt(raw[:, c, :])[:, :, 0:T - k],
                                                     sm_sb[:, l, c, SM_CONVW + 3 - k:SM_CONVW + 4 - k], av,
                                                     ALU.mult, ALU.add).then_inc(sems[k - 1], 1)

                def softplus_round(s):
                    dve.wait_ge(zexp_done, s + 1)
                    dve.tensor_scalar(wm1[:, :, :], zexp[:, :, :], 1.0, 1.0, ALU.add,
                                      ALU.subtract).then_inc(wm1_done, 1)

                def softplus_rest(s):
                    dve.wait_ge(wm1_done, s + 1)
                    dve.tensor_tensor(rest[:, :, :], zexp[:, :, :], wm1[:, :, :], ALU.subtract).then_inc(rest_done, 1)

                def softplus_end(s, g):
                    dve.wait_ge(rest_done, s + 1)
                    dve.wait_ge(lnw_done, s + 1)
                    dve.tensor_tensor(lp[:, :, :], rest[:, :, :], lnw[:, :, :], ALU.add).then_inc(lp_sum_done, 1)
                    dve.wait_ge(lp_sum_done, s + 1)
                    dve.scalar_tensor_tensor(lp[:, :, :], zexp[:, :, :], 0.5, lp[:, :, :], ALU.mult,
                                             ALU.max).then_inc(lp_done, 1)
                    dve.wait_ge(lp_done, s + 1)
                    for c in range(C + 1):
                        if c < C:
                            dve.scalar_tensor_tensor(dt[:, g, c, :], xdt[:, c, :], 0.0, lp[:, c, :], ALU.max,
                                                     ALU.add).then_inc(dt_done, 1)
                        if c > 0:
                            dve.wait_ge(dt_done, C * s + c)
                            dve.tensor_tensor(u[:, g, c - 1, :], dt[:, g, c - 1, :], xc[:, g, c - 1, :],
                                              ALU.mult).then_inc(u_done, 1)

                def mul(s, g, k):
                    p, c = k // C, k % C
                    n = UNITS * s + k
                    if p == 0:
                        dve.wait_ge(u_done, C * s + c + 1)
                    if c == 0:
                        dve.wait_ge(B_mm, PAIRS * s + p + 1)
                    if n >= RB:
                        dve.wait_ge(scan_done, n - RB + 1)
                    dve.tensor_tensor(uB[:, n % RB, :].rearrange("p (i n) -> p i n", i=2),
                                      u[:, g, c:c + 1, :].to_broadcast([128, 2, GT]),
                                      psB[:, (PAIRS * s + p) % 2, :].rearrange("p (i n) -> p i n", i=2),
                                      ALU.mult).then_inc(mul_done, 1)

                def scan(s, k):
                    n = UNITS * s + k
                    dve.wait_ge(dA_done, n + 1)
                    dve.wait_ge(mul_done, n + 1)
                    if n >= RH:
                        dve.wait_ge(hC_done, n - RH + 1)
                    dve.tensor_tensor_scan(hs[:, n % RH, :], dA[:, n % RA, :], uB[:, n % RB, :], 0.0,
                                           ALU.mult, ALU.add).then_inc(scan_done, 1)

                def gate(s, g):
                    dve.wait_ge(y_mm, UNITS * (s + 1))
                    if s:
                        dve.wait_ge(out_mm, s)
                    for c, bank in ((0, psY[:, 0, :].rearrange("p (c n) -> p c n", c=2)), (2, psY[:, 1:2, 0:GT])):
                        n = bank.shape[1]
                        dve.tensor_tensor(yg[:, c:c + n, :], bank, sz[:, g, c:c + n, :], ALU.mult).then_inc(yg_done, 1)

                def norm_stats(s):
                    dve.wait_ge(out_mm, s + 1)
                    for j in range(2):
                        dve.bn_stats(bst[:, j, :], psS[:, j * D:(j + 1) * D]).then_inc(bst_done, 1)
                    for j in range(2):
                        dve.wait_ge(bst_done, 2 * s + 1 + j)
                        dve.bn_aggr(mv[:, j, :], bst[:, j, :]).then_inc(mv_done, 1)

                def residual(s, l, g):
                    dve.wait_ge(nT_mm, s + 1)
                    dve.wait_ge(xTb_done, s + 1)
                    for k in range(2):
                        x = dve.scalar_tensor_tensor(xT[:, g, k, :], psT[0:DK, k * GT:(k + 1) * GT],
                                                     lngb_sb[:, l, k, 0:1], xTb[:, g, k, :], ALU.mult, ALU.add)
                    x.then_inc(xT_done, 1)

                def centre(s):
                    dve.wait_ge(mv_done, 2 * (s + 1))
                    dve.wait_ge(ld_ffn, LDFFN)
                    if s == RUNS - 1:
                        dve.wait_ge(hsum_done, 2)
                    for j in range(2):
                        dve.scalar_tensor_tensor(nrm[:, j, :], psS[:, j * D:(j + 1) * D], mv[:, j, 0:1], lng_row[:, :],
                                                 ALU.subtract, ALU.mult).then_inc(centred, 1)

                def base(g):
                    dve.wait_ge(xback_mm, g + 1)
                    dve.tensor_tensor(xh[:, 2 * g:2 * g + 2, :],
                                      x_bank[g][:, 0:2 * D].rearrange("p (j d) -> p j d", j=2),
                                      h0[:, g, :, :], ALU.add).then_inc(xh_done, 1)

                def h_sum(s, g):
                    dve.wait_ge(rstd_done, s + 1)
                    dve.wait_ge(centred, 2 * (g + 1))
                    dve.wait_ge(xh_done, g + 1)
                    for j in range(2):
                        dve.scalar_tensor_tensor(hsum[:, 2 * g + j, :], nrm[:, j, :], rstd[:, j:j + 1],
                                                 xh[:, 2 * g + j, :], ALU.mult, ALU.add).then_inc(hsum_done, 1)

                dve.memset(zeros[:, :], 0.0).then_inc(zeros_set, 1)
                dve.memset(dA[:, :, :], 0.0).then_inc(dA_zero, 1)
                dve.wait_ge(ld_const, 48)
                dve.wait_ge(ld_sm, 48)
                dve.tensor_scalar(acap_sb[:, :, :, :], alog_sb[:, :, :, :], A_LOG_MAX, None,
                                  ALU.min).then_inc(acap_done, 1)
                tok_out(0)
                conv_taps(0, 0, (0, 1))
                conv_taps(0, 0, (2,))
                tok_out(1)
                softplus_round(0)
                softplus_rest(0)
                softplus_end(0, 0)
                for s in range(RUNS):
                    l, g = s // 2, s % 2
                    q = s + 1
                    ql, qg = q // 2, q % 2
                    mul(s, g, 0)
                    for k in range(UNITS):
                        if k + 1 < UNITS:
                            mul(s, g, k + 1)
                        scan(s, k)
                        if s == RUNS - 1:
                            if k == LAST_DVE['gate']:
                                gate(s - 1, 0)
                            if k == LAST_DVE['stats']:
                                norm_stats(s - 1)
                            if k == LAST_DVE['centre']:
                                centre(s - 1)
                            if k == LAST_DVE['sum_0']:
                                base(0)
                                h_sum(s - 1, 0)
                            if k == LAST_DVE['base_1']:
                                base(1)
                            if k == LAST_DVE['h_stats']:
                                h_stats(dve, 0)
                            if k == LAST_DVE['h_norm']:
                                h_norm(dve, 0)
                            if k == LAST_DVE['h_parts']:
                                h_parts(dve, 0)
                        elif s > 0:
                            pl = (s - 1) // 2
                            if k == AT_DVE['gate']:
                                gate(s - 1, 1 - g)
                            if k == AT_DVE['stats']:
                                norm_stats(s - 1)
                            if k == AT_DVE['norm']:
                                residual(s - 1, pl, 1 - g)
                        if q < RUNS:
                            if k == AT_DVE['conv_a']:
                                conv_taps(q, ql, (0, 1))
                            if k == AT_DVE['conv_b']:
                                conv_taps(q, ql, (2,))
                            if k == AT_DVE['round']:
                                softplus_round(q)
                            if k == AT_DVE['rest']:
                                softplus_rest(q)
                            if k == AT_DVE['end']:
                                softplus_end(q, qg)
                s = RUNS - 1
                gate(s, 1)
                norm_stats(s)
                centre(s)
                h_sum(s, 1)

            @block.gpsimd
            def _(pool):
                pool.memset(mhalf[:, :], -0.5).then_inc(mhalf_set, 1)

                def res_bias(s, l, g):
                    pool.wait_ge(xT_done, s + 1)
                    if s == 0:
                        pool.wait_ge(tok_mm, 2)
                    pool.wait_ge(ld_sm, 48)
                    pool.tensor_tensor(xTb[:, g, :, :], xT[:, g, :, :],
                                       lngb_sb[:, l, :, 1:2].to_broadcast([DK, 2, GT]), ALU.add).then_inc(xTb_done, 1)

                def norm_scale(s):
                    pool.wait_ge(mv_done, 2 * (s + 1))
                    if s:
                        pool.wait_ge(nrm_done, 2 * s)
                    pool.tensor_scalar(vpe[:, :], mv[:, :, 1], EPS, None, ALU.add).then_inc(vpe_done, 1)
                    pool.tensor_scalar(nmean[:, :], mv[:, :, 0], -1.0, None, ALU.mult).then_inc(nmean_done, 1)
                    pool.wait_ge(vpe_done, s + 1)
                    pool.tensor_tensor(rstd[:, :], vpe[:, :], mhalf[:, 0:2], ALU.pow).then_inc(rstd_done, 1)
                    pool.wait_ge(rstd_done, s + 1)
                    pool.wait_ge(nmean_done, s + 1)
                    pool.tensor_tensor(nmr[:, :], nmean[:, :], rstd[:, :], ALU.mult).then_inc(nmr_done, 1)

                def norm_scale_only(s):
                    pool.wait_ge(mv_done, 2 * (s + 1))
                    if s == RUNS - 2:
                        pool.wait_ge(nrm_done, 2 * s)
                    else:
                        pool.wait_ge(hsum_done, 2)
                    pool.tensor_scalar(vpe[:, :], mv[:, :, 1], EPS, None, ALU.add).then_inc(vpe_done, 1)
                    pool.wait_ge(vpe_done, s + 1)
                    pool.tensor_tensor(rstd[:, :], vpe[:, :], mhalf[:, 0:2], ALU.pow).then_inc(rstd_done, 1)

                def split_rest(s, g):
                    pool.wait_ge(bc_hi_done, s + 1)
                    if s:
                        pool.wait_ge(bc_mid_done, s)
                        pool.wait_ge(rem2_done, s)
                    pool.tensor_tensor(rem[:, :], BCf[:, :], BC[:, g, :], ALU.subtract).then_inc(rem_done, 1)

                def split_rest2(s, g):
                    pool.wait_ge(bc_mid_done, s + 1)
                    if s:
                        pool.wait_ge(bc_lo_done, s)
                    pool.tensor_tensor(rem2[:, :], rem[:, :], BC[:, g, :], ALU.subtract).then_inc(rem2_done, 1)

                def times_C(s, k):
                    p, c = k // C, k % C
                    n = UNITS * s + k
                    pool.wait_ge(scan_done, n + 1)
                    if c == 0:
                        pool.wait_ge(Cb_done, PAIRS * s + p + 1)
                    if n >= RC:
                        pool.wait_ge(y_mm, n - RC + 1)
                    pool.tensor_tensor(hC[:, n % RC, :], hs[:, n % RH, :], Cb[:, (PAIRS * s + p) % RCB, :],
                                       ALU.mult).then_inc(hC_done, 1)

                pool.wait_ge(mhalf_set, 1)
                pool.wait_ge(ld_sm, 48)
                pool.wait_ge(ld_const, 48)
                for l in range(LAYERS):
                    for c in range(C):
                        pool.tensor_tensor(dpd[:, l, c, :], ident[:, :],
                                           sm_sb[:, l, c, SM_DP:SM_DP + 1].to_broadcast([128, 128]),
                                           ALU.mult).then_inc(dpd_done, 1)
                split_rest(0, 0)
                split_rest2(0, 0)
                for s in range(RUNS):
                    l, g = s // 2, s % 2
                    for k in range(UNITS):
                        times_C(s, k)
                        if k == AT_POOL['res_bias']:
                            res_bias(s, l, g)
                        if 0 < s < RUNS - 1 and k == AT_POOL['rstd']:
                            norm_scale(s - 1)
                        if s == RUNS - 1 and k == LAST_POOL['rstd']:
                            norm_scale_only(s - 1)
                        if s == RUNS - 1 and k == LAST_POOL['h_scale']:
                            h_scale(pool, 0)
                        if s + 1 < RUNS and k == AT_POOL['split_a']:
                            split_rest(s + 1, 1 - g)
                        if s + 1 < RUNS and k == AT_POOL['split_b']:
                            split_rest2(s + 1, 1 - g)
                norm_scale_only(RUNS - 1)

        stack_ctx.close()
        wi_hi, wi_lo = sb("wi_hi", [128, 2, 2, F], fp32r), sb("wi_lo", [128, 2, F], fp32r)
        wo_hl = sb("wo_hl", [128, 2, FC, 2, D], fp32r)
        top = sb("top", [128, TC, 8])
        topi = sb("topi", [128, TC, 8], u32)
        topf = sb("topf", [128, TC, 8])
        gap = sb("gap", [128, TC])
        egap = sb("egap", [128, TC])
        den = sb("den", [128, TC])
        wtop = sb("wtop", [128, 2, TC])
        gw = sb("gw", [128, TC, E])
        gw2 = sb("gw2", [128, TC, E])
        gate = sb("gate", [128, TC, E])
        gate_hl = sb("gate_hl", [128, TC, 2 * E], fp32r)
        gateT = sb("gateT", [2 * E, NTOK])
        gateTr = sb("gateTr", [2 * E, NTOK], fp32r)
        pick = sb("pick", [2 * E, E, 128], fp32r)
        gateB = sb("gateB", [128, 2, NTOK])
        RG = 8
        hg = sb("hg", [128, RG, NTOK])
        hgw = sb("hgw", [128, RG, NTOK])
        hg_hi, hg_lo = sb("hg_hi", [128, RG, NTOK], fp32r), sb("hg_lo", [128, RG, NTOK], fp32r)
        facc = sb("facc", [128, TC, D])
        facc2 = sb("facc2", [128, TC, D])
        fout = sb("fout", [128, TC, D])

        up = [psY[:, 0, :], psY[:, 1, :], psB[:, 0, :], psB[:, 1, :]]
        RU = len(up)
        down = [psU[:, :], psS[:, :], psC[:, :], psT[:, :]]

        M = E * FC
        LAGD = FC
        R64 = D - 128

        AHEAD = 4

        def item(m):
            return m + m // FC + (1 if m >= AHEAD else 0)

        def gate_item(e):
            return (FC + 1) * e if e else AHEAD

        with nc.Block() as block:

            @block.sync
            def _(sp):
                for e in range(2, E):
                    sp.wait_ge(wi_split, 3 * (e - 1))
                    sp.dma_start(wi_sb[:, e % 2, :, :], wi[e]).then_inc(ld_wi[e % 2], 16)
                    sp.wait_ge(wo_split, 2 * (e - 1))
                    sp.dma_start(wo_sb[:, e % 2, :, :], wo[e]).then_inc(ld_wo[e % 2], 16)
                for g in range(2):
                    sp.wait_ge(fin_done, 2 * (g + 1))
                    sp.dma_start(out.rearrange("(j p) d -> p j d", p=128)[:, 2 * g:2 * g + 2, :],
                                 fout[:, 2 * g:2 * g + 2, :]).then_inc(out_done, 16)
                sp.wait_ge(out_done, 2 * 16)

            @block.tensor
            def _(pe):
                def logits(g):
                    pe.wait_ge(hT_done, g + 1)
                    for j in range(2 * g, 2 * g + 2):
                        pe.matmul(psC[:, j * E:(j + 1) * E], hT[:, 0, j * 128:(j + 1) * 128], wr_sb[:, 0, :],
                                  start=True, stop=False)
                        mm = pe.matmul(psC[:, j * E:(j + 1) * E], hT[0:R64, 1, j * 128:(j + 1) * 128],
                                       wr_sb[0:R64, 1, :], start=False, stop=True)
                    mm.then_inc(logit_mm, 1)

                def up_proj(m):
                    e, f = m // FC, m % FC
                    n = item(m)
                    if f == 0:
                        pe.wait_ge(wi_split, 3 * (e + 1))
                    if m == 0:
                        pe.wait_ge(hT_split, 4)
                    if n >= RU:
                        pe.wait_ge(up_read, n - RU + 1)
                    hi, lo = wi_hi[:, e % 2, :, f * 128:(f + 1) * 128], wi_lo[:, e % 2, f * 128:(f + 1) * 128]
                    bank = up[n % RU]
                    pe.matmul(bank, hi[:, 0, :], hT_hi[:, 0, :], start=True, stop=False)
                    pe.matmul(bank, hi[:, 0, :], hT_lo[:, 0, :], start=False, stop=False)
                    pe.matmul(bank, lo, hT_hi[:, 0, :], start=False, stop=False)
                    pe.matmul(bank, hi[:, 1, :], hT_hi[:, 1, :], start=False, stop=False)
                    pe.matmul(bank, hi[0:R64, 1, :], hT_lo[0:R64, 1, :], start=False, stop=True).then_inc(up_mm, 1)

                def gate_rows(e):
                    n = gate_item(e)
                    pe.wait_ge(up_read, n - RU + 1)
                    pe.matmul(up[n % RU], pick[:, e, :], gateTr[:, :], start=True, stop=True).then_inc(up_mm, 1)

                def down_proj(m):
                    e, f = m // FC, m % FC
                    if f == 0:
                        pe.wait_ge(wo_split, 2 * (e + 1))
                    pe.wait_ge(hg_split, m + 1)
                    for j in range(TC):
                        tok = slice(j * 128, (j + 1) * 128)
                        pe.matmul(down[j][:, 0:2 * D], hg_hi[:, m % RG, tok],
                                  wo_hl[:, e % 2, f, :, :].rearrange("p a d -> p (a d)"),
                                  start=False, stop=False, skip_group_check=True)
                        mm = pe.matmul(down[j][:, 0:D], hg_lo[:, m % RG, tok], wo_hl[:, e % 2, f, 0, :],
                                       start=False, stop=(m == M - 1), skip_group_check=True)
                        if m == M - 1:
                            mm.then_inc(y_all, 1)
                    if m < M - 1:
                        mm.then_inc(down_mm, 1)

                def keep_busy(n):
                    for i in range(n):
                        pe.matmul(psB[:, 1, :], zeros[:, 0:128], zeros[:, :], start=True, stop=True)

                keep_busy(10)
                h_transposes(pe, 1)
                pe.wait_ge(ld_ffn, LDFFN)
                logits(0)
                keep_busy(6)
                up_proj(0)
                logits(1)
                for m in range(1, AHEAD):
                    up_proj(m)
                pe.wait_ge(gate_split, 2)
                for j in range(TC):
                    mm = pe.transpose(psT[0:2 * E, j * 128:(j + 1) * 128], gate_hl[:, j, :].bitcast(fp32), ident[:, :])
                mm.then_inc(gateT_mm, 1)
                for j in range(TC - 1):
                    pe.matmul(down[j], zeros[:, 0:128], zeros[:, :], start=True, stop=False, skip_group_check=True)
                pe.wait_ge(pick_done, 1)
                pe.wait_ge(gateT_done, 1)
                gate_rows(0)
                for m in range(AHEAD, FC):
                    up_proj(m)
                gate_rows(1)
                pe.wait_ge(gateT_done, 2)
                pe.matmul(down[TC - 1], zeros[:, 0:128], zeros[:, :], start=True, stop=False, skip_group_check=True)
                for j in range(TC):
                    pe.matmul(down[j][:, 0:D], gateT[:, j * 128:(j + 1) * 128], bo_sb[:, :],
                              start=False, stop=False, skip_group_check=True)
                for m in range(FC, M + LAGD):
                    if m < M:
                        if m % FC == 0 and m > FC:
                            gate_rows(m // FC)
                        up_proj(m)
                    down_proj(m - LAGD)

            @block.scalar
            def _(act):
                act.wait_ge(ld_wi[0], 16)
                act.activation(wi_hi[:, 0, :, :], wi_sb[:, 0, :, :], ACT.Copy).then_inc(wi_split, 1)
                h_copy(act, 1)
                act.wait_ge(gap_done, 1)
                act.activation(egap[:, :], gap[:, :], ACT.Exp).then_inc(egap_done, 1)

                def gelu(m):
                    e, f = m // FC, m % FC
                    n = item(m)
                    act.wait_ge(up_mm, n + 1)
                    if m >= RG:
                        act.wait_ge(gated, m - RG + 1)
                    act.activation(hg[:, m % RG, :], up[n % RU], ACT.Gelu,
                                   bias=bi_sb[:, e, f:f + 1]).then_inc(up_read, 1)

                def gate_out(e):
                    n = gate_item(e)
                    act.wait_ge(up_mm, n + 1)
                    if e >= 2:
                        act.wait_ge(gated, FC * (e - 1))
                    act.activation(gateB[:, e % 2, :], up[n % RU], ACT.Copy).then_inc(up_read, 1)

                def hidden_hi(m):
                    act.wait_ge(gated, m + 1)
                    if m >= RG:
                        act.wait_ge(down_mm, m - RG + 1)
                    act.activation(hg_hi[:, m % RG, :], hgw[:, m % RG, :], ACT.Copy).then_inc(hghi_done, 1)

                for m in range(AHEAD):
                    gelu(m)
                act.wait_ge(gateT_mm, 1)
                act.activation(gateTr[:, :], psT[0:2 * E, :], ACT.Copy).then_inc(gateT_done, 1)
                act.activation(gateT[:, :], psT[0:2 * E, :], ACT.Copy).then_inc(gateT_done, 1)
                gate_out(0)
                for m in range(AHEAD, FC):
                    gelu(m)
                gate_out(1)
                nxt = 0
                for m in range(FC, M + 2):
                    upto = min(m - 2, 2 * (m - FC) + 1)
                    while nxt <= upto:
                        hidden_hi(nxt)
                        nxt += 1
                    if m < M:
                        if m % FC == 0 and m > FC:
                            gate_out(m // FC)
                        gelu(m)

            @block.vector
            def _(dve):
                def split_wi(e, part):
                    sl = e % 2
                    if part == 0:
                        dve.wait_ge(ld_wi[sl], 16 * (e // 2 + 1))
                        if e >= 2:
                            dve.wait_ge(up_mm, item(FC * (e - 1) - 1) + 1)
                        dve.tensor_copy(wi_hi[:, sl, :, :], wi_sb[:, sl, :, :]).then_inc(wi_split, 1)
                    elif part == 1:
                        dve.wait_ge(wi_split, 3 * e + 1)
                        dve.tensor_tensor(wi_lo[:, sl, :], wi_sb[:, sl, 0, :], wi_hi[:, sl, 0, :].bitcast(fp32),
                                          ALU.subtract).then_inc(wi_split, 1)
                    else:
                        dve.tensor_tensor(wi_hi[64:128, sl, 1, :], wi_sb[64:128, sl, 1, :],
                                          wi_hi[64:128, sl, 1, :].bitcast(fp32), ALU.subtract).then_inc(wi_split, 1)

                def split_wo(e, part):
                    sl = e % 2
                    if part == 0:
                        dve.wait_ge(ld_wo[sl], 16 * (e // 2 + 1))
                        if e >= 2:
                            dve.wait_ge(down_mm, FC * (e - 1))
                        dve.tensor_copy(wo_hl[:, sl, :, 0, :], wo_sb[:, sl, :, :]).then_inc(wo_split, 1)
                    else:
                        dve.wait_ge(wo_split, 2 * e + 1)
                        dve.tensor_tensor(wo_hl[:, sl, :, 1, :], wo_sb[:, sl, :, :],
                                          wo_hl[:, sl, :, 0, :].bitcast(fp32), ALU.subtract).then_inc(wo_split, 1)

                h_stats(dve, 1)
                split_wi(0, 1)
                h_norm(dve, 1)
                split_wi(0, 2)
                h_parts(dve, 1)
                for part in range(2):
                    split_wo(0, part)
                dve.tensor_tensor(pick[:, :, :], ident[0:2 * E, 0:E].unsqueeze(2).to_broadcast([2 * E, E, 128]),
                                  ident[0:2 * E, E:2 * E].unsqueeze(2).to_broadcast([2 * E, E, 128]),
                                  ALU.add).then_inc(pick_done, 1)
                split_wi(1, 0)

                dve.wait_ge(logit_mm, 2)
                for j in range(TC):
                    dve.max(top[:, j, :], psC[:, j * E:(j + 1) * E]).then_inc(top_done, 1)
                for j in range(TC):
                    dve.wait_ge(top_done, j + 1)
                    dve.max_index(topi[:, j, :], top[:, j, :], psC[:, j * E:(j + 1) * E]).then_inc(topi_done, 1)
                dve.tensor_tensor(gap[:, :], top[:, :, 1], top[:, :, 0], ALU.subtract).then_inc(gap_done, 1)
                dve.wait_ge(topi_done, TC)
                dve.tensor_copy(topf[:, :, :], topi[:, :, :]).then_inc(topf_done, 1)
                dve.wait_ge(egap_done, 1)
                dve.tensor_scalar(den[:, :], egap[:, :], 1.0, None, ALU.add).then_inc(den_done, 1)
                dve.wait_ge(den_done, 1)
                dve.reciprocal(wtop[:, 0, :], den[:, :]).then_inc(w1_done, 1)
                dve.wait_ge(w1_done, 1)
                dve.tensor_tensor(wtop[:, 1, :], egap[:, :], wtop[:, 0, :], ALU.mult).then_inc(w2_done, 1)
                dve.wait_ge(w2_done, 1)
                dve.wait_ge(topf_done, 1)
                dve.wait_ge(ld_ffn, 64)
                for i, dst in enumerate((gw, gw2)):
                    for j in range(TC):
                        dve.tensor_scalar(dst[:, j, :], iota_sb[:, :], topf[:, j, i:i + 1], wtop[:, i, j:j + 1],
                                          ALU.is_equal, ALU.mult).then_inc(gw_done, 1)
                dve.wait_ge(gw_done, 2 * TC)
                dve.tensor_tensor(gate[:, :, :], gw[:, :, :], gw2[:, :, :], ALU.add).then_inc(gate_done, 1)
                dve.wait_ge(gate_done, 1)
                dve.tensor_copy(gate_hl[:, :, 0:E], gate[:, :, :]).then_inc(gate_split, 1)
                dve.wait_ge(gate_split, 1)
                dve.tensor_tensor(gate_hl[:, :, E:2 * E], gate[:, :, :], gate_hl[:, :, 0:E].bitcast(fp32),
                                  ALU.subtract).then_inc(gate_split, 1)

                for part in range(1, 3):
                    split_wi(1, part)
                for m in range(M):
                    e, f = m // FC, m % FC
                    dve.wait_ge(up_read, max(item(m), gate_item(e)) + 1)
                    if m >= RG:
                        dve.wait_ge(hg_split, m - RG + 1)
                    dve.tensor_tensor(hgw[:, m % RG, :], hg[:, m % RG, :], gateB[:, e % 2, :],
                                      ALU.mult).then_inc(gated, 1)
                    if f < 2 and e > 0:
                        split_wo(e, f)
                    if 2 <= f < 5 and 1 <= e < E - 1:
                        split_wi(e + 1, f - 2)
                for g in range(2):
                    js = range(2 * g, 2 * g + 2)
                    for j in js:
                        dve.wait_ge(y_all, j + 1)
                        dve.tensor_tensor(facc[:, j, :], down[j][:, D:2 * D], hh[:, j, 0:D],
                                          ALU.add).then_inc(facc_done, 1)
                    for j in js:
                        dve.wait_ge(facc_done, j + 1)
                        dve.tensor_tensor(facc2[:, j, :], down[j][:, 0:D], facc[:, j, :],
                                          ALU.add).then_inc(facc2_done, 1)
                    for j in js:
                        dve.wait_ge(facc2_done, j + 1)
                        dve.bn_stats(fst[:, j, :], facc2[:, j, :]).then_inc(fst_done, 1)
                    for j in js:
                        dve.wait_ge(fst_done, TC + j + 1)
                        dve.bn_aggr(fmv[:, j, :], fst[:, j, :]).then_inc(fmv_done, 1)
                for j in range(TC):
                    dve.wait_ge(frstd_done, 3 + j // 2)
                    dve.tensor_scalar(fout[:, j, :], facc2[:, j, :], fmv[:, j, 0:1], frstd[:, j:j + 1],
                                      ALU.subtract, ALU.mult).then_inc(fin_done, 1)

            @block.gpsimd
            def _(pool):
                h_scale(pool, 1)
                for m in range(M):
                    pool.wait_ge(hghi_done, m + 1)
                    if m >= RG:
                        pool.wait_ge(down_mm, m - RG + 1)
                    pool.tensor_tensor(hg_lo[:, m % RG, :], hgw[:, m % RG, :], hg_hi[:, m % RG, :].bitcast(fp32),
                                       ALU.subtract).then_inc(hg_split, 1)
                for g in range(2):
                    js = slice(2 * g, 2 * g + 2)
                    pool.wait_ge(fmv_done, TC + 2 * (g + 1))
                    pool.tensor_scalar(fvpe[:, js], fmv[:, js, 1], EPS, None, ALU.add).then_inc(fvpe_done, 1)
                    pool.wait_ge(fvpe_done, 3 + g)
                    pool.tensor_tensor(frstd[:, js], fvpe[:, js], mhalf[:, js], ALU.pow).then_inc(frstd_done, 1)


_ORDER = ["patches", "tok_w", "tok_b", "in_w", "xp_w", "dt_w", "out_w", "lngb", "smalls", "a_log",
          "wr", "wi", "bi", "wo", "bo", "eye", "sel", "iota8", "last_g"]


def kernel(**inputs):
    import numpy as _np
    import concourse.bacc as _bacc
    from concourse import mybir as _mybir
    from concourse.bass_utils import run_bass_kernel_spmd as _run

    def rows(m, k):
        m = m.reshape(m.shape[:-2] + (k, m.shape[-2] // k, m.shape[-1]))
        return _np.moveaxis(m, -3, -2)

    def on_all(m):
        return _np.repeat(m[None], 128, 0)

    i = {n: _np.asarray(v) for n, v in inputs.items()}
    at = {n[len("L0_attn_"):]: v for n, v in i.items() if n.startswith("L0_attn_")}
    ff = {n[len("L0_ffn_"):]: v for n, v in i.items() if n.startswith("L0_ffn_")}
    a = {}
    side = int(T ** 0.5)
    p = i["x"].shape[-1] // side
    pt = i["x"].reshape(B, 3, side, p, side, p).transpose(0, 2, 4, 3, 5, 1).reshape(NTOK, PATCH)
    a["patches"] = rows(pt.T, PC)
    a["tok_w"] = rows(i["L0_tok_W"].T, PC)
    a["tok_b"] = on_all(i["L0_tok_b"])
    a["in_w"] = rows(at["in_proj_w"].transpose(0, 2, 1), 2)
    xp = at["x_proj_w"]
    bc = xp[:, RANK:]
    pad = _np.zeros((LAYERS, 2 * NST - RANK, DI), xp.dtype)
    a["xp_w"] = rows(_np.concatenate([xp[:, :RANK], pad, bc, bc, bc], 1).transpose(0, 2, 1), C)
    a["dt_w"] = at["dt_proj_w"].transpose(0, 2, 1)
    a["out_w"] = rows(at["out_proj_w"].transpose(0, 2, 1), C)
    a["lngb"] = _np.stack([at["ln_g"], at["ln_b"]], -1).reshape(LAYERS, 2, DK, 2).transpose(2, 0, 1, 3)
    a["last_g"] = on_all(at["ln_g"][-1])
    small = _np.concatenate([at["conv_w"], at["conv_b"][..., None], at["dt_proj_b"][..., None],
                             at["D_param"][..., None]], -1)
    a["smalls"] = small.reshape(LAYERS, C, 128, SM).transpose(2, 0, 1, 3)
    a["a_log"] = at["A_log"].reshape(LAYERS, C, 128, NST).transpose(2, 0, 1, 3)

    def rows_128_and_rest_twice(m):
        return _np.stack([m[..., :128, :], _np.concatenate([m[..., 128:, :]] * 2, -2)], -2)

    a["wr"] = rows_128_and_rest_twice(ff["Wr"].T)
    a["wi"] = rows_128_and_rest_twice(ff["Wi"].transpose(0, 2, 1))
    a["bi"] = ff["bi"].reshape(E, FC, 128).transpose(2, 0, 1)
    a["wo"] = rows(ff["Wo"].transpose(0, 2, 1), FC)
    a["bo"] = _np.concatenate([ff["bo"]] * 2, 0)
    a["iota8"] = on_all(_np.arange(E, dtype=_np.float32))
    a["eye"] = _np.eye(128, dtype=_np.float32)
    a["sel"] = _np.concatenate([_np.zeros((32, 32), _np.float32)] + 3 * [_np.eye(32, dtype=_np.float32)], 0)

    nc = _bacc.Bacc("TRN2", target_bir_lowering=False, num_devices=1)
    arrays, args = {}, []
    for n in _ORDER:
        arrays[f"in_{n}_dram"] = _np.ascontiguousarray(a[n])
        args.append(nc.dram_tensor(f"in_{n}_dram", a[n].shape, _mybir.dt.from_np(a[n].dtype),
                                   kind="ExternalInput").ap())
    args.append(nc.dram_tensor("out_0_dram", (NTOK, D), _mybir.dt.float32, kind="ExternalOutput").ap())
    tower_program(nc, *args)
    r = _run(nc, [arrays], core_ids=[0])
    return r.results[0]["out_0_dram"].reshape(B, T, D)
```
